# Optimizing a Trainium2 kernel written in Bass

```python
import numpy as np
import jax
import jax.numpy as jnp

def _softmax(x, axis=-1):
    return jax.nn.softmax(x, axis=axis)

def _gelu(x):
    return jax.nn.gelu(x, approximate=True)

def _silu(x):
    return jax.nn.silu(x)

def _sigmoid(x):
    return jax.nn.sigmoid(x)

def _layernorm(x, axis=-1, eps=1e-05):
    m = jnp.mean(x, axis=axis, keepdims=True)
    v = jnp.var(x, axis=axis, keepdims=True)
    return (x - m) / jnp.sqrt(v + eps)

def _scatter_add(tgt, idx, src, axis=0):
    return tgt.at[idx].add(src)

def _segment_sum(src, seg, n):
    return jax.ops.segment_sum(src, seg, n)
kernel_name = 'mk_gnn_resnorm_d1_gnn_r32_07c37c'

def setup_inputs(seed: int=0):
    np.random.seed(seed)
    _w = jnp.asarray

    def _rec_inputs():
        import jax
        import jax.numpy as jnp
        _gk = jax.random.key(seed)
        x = -0.000202 + 1 * jax.random.normal(jax.random.fold_in(_gk, 1), (50000, 128), jnp.float32)
        src = jax.random.randint(jax.random.fold_in(_gk, 2), (25000,), 0, 50000, jnp.int32)
        dst = jnp.minimum((50000 * jax.random.uniform(jax.random.fold_in(_gk, 3), (25000,)) ** 2.0).astype(jnp.int32), 49999)
        _o = jnp.argsort(dst, stable=True)
        src = src[_o]
        dst = dst[_o]
        return (x, src, dst)
    x, src, dst = _rec_inputs()

    def _L0_gnn_setup():
        import jax, jax.numpy as jnp
        import numpy as np
        N, E, D, H = (50000, 25000, 128, 4)
        DH = D // H
        BN_EPS = 1e-05
        key = jax.random.key(seed)
        ks = jax.random.split(key, 16)
        s = 0.02
        inp = {'x': jax.random.normal(ks[0], (N, D), dtype=jnp.float32), 'edge_index': jax.random.randint(ks[1], (2, E), 0, N, dtype=jnp.int64), 'Wk': jax.random.normal(ks[2], (D, D), dtype=jnp.float32) * s, 'bk': jnp.zeros((D,), jnp.float32), 'Wm': jax.random.normal(ks[3], (D, D), dtype=jnp.float32) * s, 'bm': jnp.zeros((D,), jnp.float32), 'Wq': jax.random.normal(ks[4], (D, D), dtype=jnp.float32) * s, 'bq': jnp.zeros((D,), jnp.float32), 'W1': jax.random.normal(ks[5], (D, D), dtype=jnp.float32) * s, 'b1': jnp.zeros((D,), jnp.float32), 'gamma': jnp.ones((D,), jnp.float32), 'beta': jnp.zeros((D,), jnp.float32), 'W2': jax.random.normal(ks[6], (D, D), dtype=jnp.float32) * s, 'b2': jnp.zeros((D,), jnp.float32)}
        return inp
    _L0_gnn_all = _L0_gnn_setup()
    _L0_gnn_in = {k: v for k, v in _L0_gnn_all.items() if k in ('Wk', 'bk', 'Wm', 'bm', 'Wq', 'bq', 'W1', 'b1', 'gamma', 'beta', 'W2', 'b2')}
    del _L0_gnn_all
    return {'x': x, 'src': src, 'dst': dst, 'L0_gnn_Wk': _L0_gnn_in['Wk'], 'L0_gnn_bk': _L0_gnn_in['bk'], 'L0_gnn_Wm': _L0_gnn_in['Wm'], 'L0_gnn_bm': _L0_gnn_in['bm'], 'L0_gnn_Wq': _L0_gnn_in['Wq'], 'L0_gnn_bq': _L0_gnn_in['bq'], 'L0_gnn_W1': _L0_gnn_in['W1'], 'L0_gnn_b1': _L0_gnn_in['b1'], 'L0_gnn_gamma': _L0_gnn_in['gamma'], 'L0_gnn_beta': _L0_gnn_in['beta'], 'L0_gnn_W2': _L0_gnn_in['W2'], 'L0_gnn_b2': _L0_gnn_in['b2']}

def reference(x, src, dst, L0_gnn_Wk, L0_gnn_bk, L0_gnn_Wm, L0_gnn_bm, L0_gnn_Wq, L0_gnn_bq, L0_gnn_W1, L0_gnn_b1, L0_gnn_gamma, L0_gnn_beta, L0_gnn_W2, L0_gnn_b2):
    import jax
    import jax.numpy as jnp

    def _L0_gnn_ref(x, edge_index, Wk, bk, Wm, bm, Wq, bq, W1, b1, gamma, beta, W2, b2):
        import jax, jax.numpy as jnp
        import numpy as np
        N, E, D, H = (50000, 25000, 128, 4)
        DH = D // H
        BN_EPS = 1e-05
        src = edge_index[0]
        dst = edge_index[1]
        x_i = x[dst]
        x_j = x[src]
        key = (x_i @ Wk + bk).reshape(-1, H, DH)
        msg = (x_j @ Wm + bm).reshape(-1, H, DH)
        query = (x_j @ Wq + bq).reshape(-1, H, DH) / jnp.sqrt(jnp.float32(DH))
        scores = jnp.sum(query * key, axis=2)
        smax = jax.ops.segment_max(scores, src, num_segments=N)
        e = jnp.exp(scores - smax[src])
        ssum = jax.ops.segment_sum(e, src, num_segments=N)
        alpha = e / ssum[src]
        cnt = jax.ops.segment_sum(jnp.ones((scores.shape[0],), jnp.float32), src, num_segments=N)
        alpha = alpha * cnt[src][:, None]
        out_e = (msg * alpha[:, :, None]).reshape(-1, D)
        out = jax.ops.segment_sum(out_e, dst, num_segments=N)
        h = out @ W1 + b1
        mean = jnp.mean(h, axis=0)
        var = jnp.var(h, axis=0)
        h = (h - mean) * jax.lax.rsqrt(var + BN_EPS) * gamma + beta
        h = jax.nn.relu(h)
        return h @ W2 + b2
    edge_index = jnp.stack([src, dst])
    x = _layernorm(x + _L0_gnn_ref(x, edge_index, L0_gnn_Wk, L0_gnn_bk, L0_gnn_Wm, L0_gnn_bm, L0_gnn_Wq, L0_gnn_bq, L0_gnn_W1, L0_gnn_b1, L0_gnn_gamma, L0_gnn_beta, L0_gnn_W2, L0_gnn_b2), axis=-1)
    return x

_drawn_inputs = setup_inputs


def setup_inputs(seed=0):
    import zlib

    import numpy as np

    out = dict(_drawn_inputs(seed))
    spreads = {'L0_gnn_bk': (0.0, 0.8),
     'L0_gnn_bm': (0.0, 0.1),
     'L0_gnn_bq': (0.0, 0.8),
     'L0_gnn_b1': (0.0, 0.8),
     'L0_gnn_gamma': (1.0, 0.547),
     'L0_gnn_beta': (0.0, 0.503),
     'L0_gnn_b2': (0.0, 0.1)}
    factors = {'L0_gnn_Wk': 8.0, 'L0_gnn_Wq': 8.0}
    for name, (base, spread) in spreads.items():
        noise = np.random.default_rng([zlib.crc32(name.encode()), seed]).standard_normal(out[name].shape)
        drawn = base * np.exp(spread * noise) if base else spread * noise
        out[name] = jnp.asarray(drawn.astype(out[name].dtype))
    for name, factor in factors.items():
        out[name] = (out[name] * factor).astype(out[name].dtype)
    return out
```

```python
import math
from contextlib import ExitStack

import concourse.bass as bass
from concourse import mybir

F32 = mybir.dt.float32
BF16 = mybir.dt.bfloat16
I32 = mybir.dt.int32
U16 = mybir.dt.uint16
ALU = mybir.AluOpType
ACT = mybir.ActivationFunctionType
AX = mybir.AxisListType

N = 50000
E = 25000
D = 128
H = 4
DH = D // H
EPS = 1e-5
P = 128
TILES = -(-E // P)
U = 7
GROUPS = TILES // U
PAIRS = GROUPS // 2
GW = U * P
ROWS = TILES * P
SORT = 256
SR = TILES // 2
LP, LC = 125, 200
NPP = 390
CN = 13
CHUNKS = NPP // CN
RINGD = 3
CW = CN * D
TAIL = N - P * NPP
LOW = -1.0e30
SKIP = 100000
HALF = N // 2


def build(nc, x, src, dst, Wk, bk, Wm, bm, Wq, bq, W1, b1, gamma, beta, W2, b2, y, DEBUG=None):
    ctx = ExitStack()
    with ctx:
        def sb(name, shape, dt=F32):
            return ctx.enter_context(nc.sbuf_tensor(name, shape, dt))

        def sem(name):
            return ctx.enter_context(nc.semaphore(name))

        xdst_d = nc.dram_tensor("xdst_d", [GROUPS, P, GW], F32).ap()
        scores_d = nc.dram_tensor("scores_d", [ROWS, H], F32).ap()
        alpha_d = nc.dram_tensor("alpha_d", [ROWS, H], F32).ap()
        same_d = nc.dram_tensor("same_d", [P * SORT], BF16).ap()

        ident = sb("ident", [P, P])
        down = sb("down", [P, P])
        up = sb("up", [P, P])
        heads = sb("heads", [P, H])
        wk, wq, wm, w1, w2 = (sb(n, [P, D]) for n in ("wk", "wq", "wm", "w1", "w2"))
        bkc, bqc, b1c, gammac, betac = (sb(n, [P, 1]) for n in ("bkc", "bqc", "b1c", "gammac", "betac"))
        bmr = sb("bmr", [P, D])
        b2r = sb("b2r", [P, D])
        epsc = sb("epsc", [P, 1])
        sign_i = sb("sign_i", [P, 2], I32)
        signs = sb("signs", [P, 6])
        turn = sb("turn", [P, 5, SORT])
        place = sb("place", [P, SORT])

        big = sb("big", [P, ROWS])
        dst_i = sb("dst_i", [P, TILES], I32)
        src_i = sb("src_i", [P, TILES], I32)
        out_i = sb("out_i", [P, TILES], I32)
        row_i = sb("row_i", [P, TILES], I32)
        stage = sb("stage", [P, 2, U], I32)
        rows = sb("rows", [P, 2, GW])
        ringA = sb("ringA", [P, 2, GW])
        ringB = sb("ringB", [P, 2, GW])
        flags = sb("flags", [P, 2, GW + 2], BF16)
        small = sb("small", [P, 2, U * H])
        sc = sb("sc", [P, TILES * H])
        gs = sb("gs", [P, H, TILES])
        sums = sb("sums", [P, 2, GROUPS])
        bn = sb("bn", [P, 12])
        rest = sb("rest", [P, D])
        lnst = sb("lnst", [P, RINGD, CN * 6])
        lnsm = sb("lnsm", [P, RINGD, 8, CN])

        room = sb("room", [P, 2 * RINGD * CW])
        used = [0]

        def take(n):
            used[0] += n
            assert used[0] <= 2 * RINGD * CW
            return room[:, used[0] - n:used[0]]

        va, vb, t1, t2 = (take(SORT) for _ in range(4))
        key, pay, key1 = (take(SORT) for _ in range(3))
        same1 = take(SORT + 1)
        same2 = take(SORT + 1)
        same16 = take(SORT // 2).bitcast(BF16)
        raw = take(2 * LC).bitcast(I32)
        seg = take((H + 1) * SORT)
        fwd = take((H + 1) * SORT)
        bwd = take((H + 1) * SORT)
        negs = take(SORT)
        pack = take(12)
        crow = take(2 * P)
        cscan = take(P + 2)
        carry = take(8)
        xin = [room[:, i * CW:(i + 1) * CW] for i in range(RINGD)]
        xout = [room[:, (RINGD + i) * CW:(RINGD + i + 1) * CW] for i in range(RINGD)]

        PS = [ctx.enter_context(nc.psum_tensor(f"ps{i}", [P, 1024], F32)) for i in range(4)]

        pace = {n: sem(f"pace_{n}") for n in ("sp", "pool", "act", "dve", "pe")}
        lists_in, weights_in, biases_in = sem("lists_in"), sem("weights_in"), sem("biases_in")
        consts = sem("consts")
        dve_step, act_step, pe_step, pool_step = sem("dve_step"), sem("act_step"), sem("pe_step"), sem("pool_step")
        sorted_keys = sem("sorted_keys")
        shifted = sem("shifted")
        marks = sem("marks")
        turned = sem("turned")
        indexed = sem("indexed")
        marks_out = sem("marks_out")
        kd_in = [sem(f"kd_in{h}") for h in range(2)]
        kd_saved = [sem(f"kd_saved{h}") for h in range(2)]
        kd_turned = sem("kd_turned")
        kx_ready = sem("kx_ready")
        k_made = sem("k_made")
        k_kept = sem("k_kept")
        qs_in = [sem(f"qs_in{h}") for h in range(2)]
        qs_turned = sem("qs_turned")
        qx_ready = sem("qx_ready")
        q_made = sem("q_made")
        qk_ready = sem("qk_ready")
        m_made = sem("m_made")
        m_kept = sem("m_kept")
        s_made = sem("s_made")
        s_kept = sem("s_kept")
        scores_out = sem("scores_out")
        g_in = [sem(f"g_in{h}") for h in range(2)]
        g_kept = sem("g_kept")
        soft_pe = sem("soft_pe")
        soft_dve = sem("soft_dve")
        soft_act = sem("soft_act")
        soft_exp = sem("soft_exp")
        weights_ready = sem("weights_ready")
        a_out = [sem(f"a_out{h}") for h in range(2)]
        alpha_in = sem("alpha_in")
        f_in = [sem(f"f_in{h}") for h in range(2)]
        o_made = sem("o_made")
        o_turned = sem("o_turned")
        run_sums = sem("run_sums")
        h_made = sem("h_made")
        h_kept = sem("h_kept")
        squares = sem("squares")
        bn_var = sem("bn_var")
        bn_sd = sem("bn_sd")
        bn_bias = sem("bn_bias")
        bn_rest = sem("bn_rest")
        rest_made = sem("rest_made")
        rest_ready = sem("rest_ready")
        d_in = [sem(f"d_in{i}") for i in range(RINGD)]
        d_out = [sem(f"d_out{i}") for i in range(RINGD)]
        d_added, d_var, d_sd, d_scale, d_done = (sem(f"d_{n}") for n in ("added", "var", "sd", "scale", "done"))
        tail_in, tail_out = sem("tail_in"), sem("tail_out")
        e_in = [sem(f"e_in{h}") for h in range(2)]
        e_relu, e_made, e_read, e_var, e_sd, e_scale, e_done = (
            sem(f"e_{n}") for n in ("relu", "made", "read", "var", "sd", "scale", "done"))
        e_out = [sem(f"e_out{h}") for h in range(2)]

        def hold(eng, name, s, value):
            if isinstance(value, int):
                if value > 0:
                    eng.wait_ge(s, value)
            else:
                eng.wait_ge(s, value)
                eng.sem_inc(pace[name], 1)

        class Steps:

            def __init__(self, eng, name, s):
                self.eng, self.name, self.sem, self.n, self.local = eng, name, s, 0, 0

            def __call__(self, ins):
                ins.then_inc(self.sem, 1)
                self.local += 1

            def settle(self):
                hold(self.eng, self.name, self.sem, self.n + self.local)

            def loop(self, eng, first, last, body):
                self.n, self.local = self.n + self.local, 0
                start = self.n
                body(first)
                self.settle()
                once = self.local
                self.local = 0
                with eng.Fori(first + 1, last) as i:
                    self.n = start + once + (i - (first + 1)) * once
                    body(i)
                    self.settle()
                    assert self.local == once, (self.local, once)
                self.n, self.local = start + (last - first) * once, 0

        def group(t, g):
            return t[:, bass.ds(g * GW, GW)]

        block = ctx.enter_context(nc.Block())

        @block.sync
        def _(sp):
            sp.dma_start(raw[0:LP, 0:LC], dst.rearrange("(p n) -> p n", p=LP)).then_inc(lists_in, 16)
            sp.dma_start(raw[0:LP, LC:2 * LC], src.rearrange("(p n) -> p n", p=LP)).then_inc(lists_in, 16)
            for t, w in ((wk, Wk), (wq, Wq), (wm, Wm), (w1, W1), (w2, W2)):
                sp.dma_start(t[:, :], w).then_inc(weights_in, 16)
            for t, b in ((bkc, bk), (bqc, bq), (b1c, b1), (gammac, gamma), (betac, beta)):
                sp.dma_start(t[:, :], b.rearrange("(p o) -> p o", o=1)).then_inc(biases_in, 16)
            for t, b in ((bmr, bm), (b2r, b2)):
                sp.dma_start(t[:, :], b.partition_broadcast(P)).then_inc(biases_in, 16)
            sp.wait_ge(indexed, 1)
            sp.dma_start(same_d.rearrange("(p n) -> p n", p=P), same16).then_inc(marks_out, 16)

            def save(i):
                for h in range(2):
                    hold(sp, "sp", kd_in[h], (i + 1) * 16 * U)
                    sp.dma_start(xdst_d[bass.ds(2 * i + h, 1), :, :].rearrange("o p n -> (o p) n"),
                                 rows[:, h, :]).then_inc(kd_saved[h], 16)
            save(0)
            with sp.Fori(1, PAIRS) as i:
                save(i)

            sp.wait_ge(s_kept, GROUPS)
            sp.dma_start(scores_d.rearrange("(p t) h -> p (t h)", p=P), sc[:, :]).then_inc(scores_out, 16)

            for h in range(2):
                sp.wait_ge(a_out[h], 16 * U * PAIRS)
            sp.dma_start(sc[:, :], alpha_d.rearrange("(p t) h -> p (t h)", p=P)).then_inc(alpha_in, 16)

            sp.wait_ge(marks_out, 16)

            def load_marks(i):
                for h in range(2):
                    g = 2 * i + h
                    hold(sp, "sp", h_kept, g - 1)
                    sp.dma_start(flags[:, h, 0:GW + 1],
                                 same_d[bass.ds(g * GW, GW + 1)].partition_broadcast(P)).then_inc(f_in[h], 16)
            load_marks(0)
            with sp.Fori(1, PAIRS) as i:
                load_marks(i)

            xv = x[0:P * NPP, :].rearrange("(p n) d -> p (n d)", p=P)
            yv = y[0:P * NPP, :].rearrange("(p n) d -> p (n d)", p=P)
            sp.wait_ge(weights_ready, 2)

            def dense(i):
                for k in range(RINGD):
                    c = RINGD * i + k
                    if not isinstance(i, int) or i > 0:
                        hold(sp, "sp", d_done, c - RINGD + 1)
                        sp.dma_start(yv[:, bass.ds((c - RINGD) * CW, CW)], xout[k]).then_inc(d_out[k], 16)
                    sp.dma_start(xin[k], xv[:, bass.ds(c * CW, CW)]).then_inc(d_in[k], 16)
            dense(0)
            with sp.Fori(1, CHUNKS // RINGD) as i:
                dense(i)
            for k in range(RINGD):
                c = CHUNKS + k
                sp.wait_ge(d_done, c - RINGD + 1)
                sp.dma_start(yv[:, (c - RINGD) * CW:(c - RINGD + 1) * CW], xout[k]).then_inc(d_out[k], 16)
                if k == 0:
                    sp.dma_start(xin[0][0:TAIL, 0:D], x[P * NPP:N, :]).then_inc(tail_in, 16)
            sp.wait_ge(d_done, CHUNKS + 1)
            sp.dma_start(y[P * NPP:N, :], xout[0][0:TAIL, 0:D]).then_inc(tail_out, 16)

            def load_rows(i):
                for h in range(2):
                    g = 2 * i + h
                    hold(sp, "sp", e_read, g - 1)
                    sp.dma_start(ringB[:, h, :],
                                 xdst_d[bass.ds(g, 1), :, :].rearrange("o p n -> (o p) n")).then_inc(e_in[h], 16)
            for h in range(2):
                sp.wait_ge(kd_saved[h], 16 * PAIRS)
            load_rows(0)
            with sp.Fori(1, PAIRS) as i:
                load_rows(i)
            for k in range(RINGD):
                sp.wait_ge(d_out[k], 16 * (CHUNKS // RINGD))
            sp.wait_ge(tail_out, 16)
            for h in range(2):
                sp.wait_ge(e_out[h], 16 * U * PAIRS)

        @block.gpsimd
        def _(pool):
            step = Steps(pool, "pool", pool_step)
            step(pool.memset(ident[:, :], 0.0))
            step(pool.memset(down[:, :], 0.0))
            step(pool.memset(up[:, :], 0.0))
            step(pool.memset(heads[:, :], 0.0))
            step(pool.memset(turn[:, :, :], 1.0))
            step(pool.memset(signs[:, :], 1.0))
            step(pool.memset(epsc[:, :], EPS))
            step(pool.iota(sign_i[:, 0:1], [[0, 1]], base=0, channel_multiplier=1))
            step(pool.iota(place[:, :].bitcast(I32), [[1, 2], [TILES, P]], base=0, channel_multiplier=2))
            step.settle()
            for m, base in ((ident, 0), (down, 1), (up, -1)):
                step(pool.affine_select(out=m[:, :], in_=m[:, :], compare_op=ALU.not_equal, fill=1.0, base=base,
                                        pattern=[[-1, P]], channel_multiplier=1))
            step.settle()
            for h in range(H):
                step(pool.memset(heads[DH * h:DH * h + DH, h:h + 1], 1.0 / math.sqrt(DH)))
                step.settle()
            for k in range(4):
                w = 2 ** k
                v = turn[:, k, :].rearrange("p (n q) -> p n q", q=4 * w)
                step(pool.memset(v[:, :, w:3 * w], -1.0))
            step(pool.memset(turn[:, 4, :].rearrange("p (n q) -> p n q", q=32)[:, :, 16:32], -1.0))
            step.settle()
            for q in range(4):
                b13, b14 = q & 1, q >> 1
                for col, s in ((1, b13), (2, b14), (3, b13 ^ b14)):
                    if s:
                        step(pool.memset(signs[32 * q:32 * q + 32, col:col + 1], -1.0))
                        step.settle()
            pool.sem_inc(consts, 1)

            staged = [0]

            def ahead(index, i, h, extra=None):
                g = 2 * i + h
                step(pool.tensor_copy(stage[:, h, :], index[:, bass.ds(g * U, U)]))
                if extra is not None:
                    step(pool.tensor_copy(small[:, h, :], extra[:, bass.ds(g * U * H, U * H)]))
                step.settle()

            def gather(i, h, table, index, out, width, done):
                ahead(index, i, h)
                for k in range(U):
                    pool.indirect_dma_start(
                        out=out[:, h, k * width:(k + 1) * width], out_offset=None, in_=table,
                        in_offset=bass.IndirectOffsetOnAxis(ap=stage[:, h, k:k + 1], axis=0)).then_inc(done[h], 16)

            pool.wait_ge(indexed, 1)

            def keys(i):
                for h in range(2):
                    hold(pool, "pool", kd_turned, 2 * i + h - 1)
                    hold(pool, "pool", kd_saved[h], i * 16)
                    gather(i, h, x[:, :], dst_i, rows, D, kd_in)
            step.loop(pool, 0, PAIRS, keys)

            pool.wait_ge(kd_turned, GROUPS)
            for h in range(2):
                pool.wait_ge(kd_saved[h], 16 * PAIRS)

            def scores(i):
                for h in range(2):
                    hold(pool, "pool", qs_turned, 2 * i + h - 1)
                    gather(i, h, x[:, :], src_i, rows, D, qs_in)
            step.loop(pool, 0, PAIRS, scores)

            pool.wait_ge(qs_turned, GROUPS)
            pool.wait_ge(indexed, 2)
            pool.wait_ge(scores_out, 16)

            def by_src(i):
                for h in range(2):
                    hold(pool, "pool", g_kept, 2 * i + h - 1)
                    gather(i, h, scores_d[:, :], row_i, small, H, g_in)
            step.loop(pool, 0, PAIRS, by_src)

            pool.wait_ge(weights_ready, 1)
            gsf = gs[:, :, :].rearrange("p h t -> p (h t)")

            def to_dst(i):
                for h in range(2):
                    hold(pool, "pool", a_out[h], i * 16 * U)
                    ahead(row_i, i, h, gsf)
                    for k in range(U):
                        pool.indirect_dma_start(
                            out=alpha_d[:, :], out_offset=bass.IndirectOffsetOnAxis(ap=stage[:, h, k:k + 1], axis=0),
                            in_=small[:, h, k * H:(k + 1) * H], in_offset=None).then_inc(a_out[h], 16)
            step.loop(pool, 0, PAIRS, to_dst)
            for h in range(2):
                pool.wait_ge(a_out[h], 16 * U * PAIRS)

            pool.wait_ge(rest_ready, 1)

            def add(i):
                for k in range(RINGD):
                    hold(pool, "pool", d_in[k], (i + 1) * 16)
                    v = xin[k].rearrange("p (n d) -> p n d", d=D)
                    pool.tensor_tensor(v, v, rest[:, :].unsqueeze(1).to_broadcast([P, CN, D]),
                                       ALU.add).then_inc(d_added, 1)
            add(0)
            with pool.Fori(1, CHUNKS // RINGD) as i:
                add(i)
            pool.wait_ge(tail_in, 16)
            pool.tensor_tensor(xin[0][0:TAIL, 0:D], xin[0][0:TAIL, 0:D], rest[0:TAIL, :], ALU.add).then_inc(d_added, 1)

            for k in range(RINGD):
                pool.wait_ge(d_out[k], 16 * (CHUNKS // RINGD))
            pool.wait_ge(tail_out, 16)

            def finals(i):
                for h in range(2):
                    hold(pool, "pool", e_out[h], i * 16 * U)
                    ahead(out_i, i, h)
                    hold(pool, "pool", e_done, 2 * i + h + 1)
                    for k in range(U):
                        pool.indirect_dma_start(
                            out=y[:, :], out_offset=bass.IndirectOffsetOnAxis(ap=stage[:, h, k:k + 1], axis=0),
                            in_=rows[:, h, k * D:(k + 1) * D], in_offset=None,
                            bounds_check=N - 1, oob_is_err=False).then_inc(e_out[h], 16)
            step.loop(pool, 0, PAIRS, finals)

        @block.scalar
        def _(act):
            step = Steps(act, "act", act_step)
            act.wait_ge(biases_in, 16 * 7)

            def keys(i):
                for h in range(2):
                    g = 2 * i + h
                    hold(act, "act", kd_turned, g + 1)
                    hold(act, "act", k_made, g - 1)
                    act.activation(ringA[:, h, :], PS[0][:, 0:GW], ACT.Identity).then_inc(kx_ready, 1)
                    hold(act, "act", k_made, g + 1)
                    act.activation(group(big, g), PS[1][:, 0:GW], ACT.Identity, bias=bkc[:, 0:1]).then_inc(k_kept, 1)
            keys(0)
            with act.Fori(1, PAIRS) as i:
                keys(i)
            act.wait_ge(k_made, GROUPS)

            def scores(i):
                for h in range(2):
                    g = 2 * i + h
                    hold(act, "act", qs_turned, g + 1)
                    hold(act, "act", m_made, g - 1)
                    act.activation(ringA[:, h, :], PS[0][:, 0:GW], ACT.Identity).then_inc(qx_ready, 1)
            scores(0)
            with act.Fori(1, PAIRS) as i:
                scores(i)

            act.wait_ge(soft_act, 1)
            act.activation(seg[0:SR, 0:H * SORT], bwd[0:SR, 0:H * SORT], ACT.Exp).then_inc(soft_exp, 1)

            def square(i):
                for h in range(2):
                    g = 2 * i + h
                    hold(act, "act", h_kept, g + 1)
                    step.settle()
                    step(act.activation(rows[:, h, :], group(big, g), ACT.Square,
                                        accum_out=sums[:, 1, bass.ds(g, 1)]))
                    act.sem_inc(pace["act"], 1)
            step.loop(act, 0, PAIRS, square)
            step.settle()
            act.sem_inc(squares, 1)

            act.wait_ge(bn_var, 1)
            act.activation(bn[:, 3:4], bn[:, 2:3], ACT.Sqrt, bias=epsc[:, 0:1]).then_inc(bn_sd, 1)
            act.wait_ge(bn_bias, 1)
            act.activation(bn[:, 8:9], bn[:, 7:8], ACT.Relu).then_inc(bn_rest, 1)

            def normalise(n, k, p, data, out, done):
                for j in range(n):
                    ins = act.activation(out[0:p, j * D:(j + 1) * D], data[0:p, j * D:(j + 1) * D], ACT.Identity,
                                         bias=lnsm[0:p, k, 6, j:j + 1], scale=lnsm[0:p, k, 5, j:j + 1])
                ins.then_inc(done, 1)

            def root(n, k, p, sd):
                act.activation(lnsm[0:p, k, 4, 0:n], lnsm[0:p, k, 3, 0:n], ACT.Sqrt, scale=1.0 / D,
                               bias=epsc[0:p, 0:1]).then_inc(sd, 1)

            def dense(i):
                for k in range(RINGD):
                    c = RINGD * i + k
                    hold(act, "act", d_var, c + 1)
                    root(CN, k, P, d_sd)
                    hold(act, "act", d_scale, c + 1)
                    if not isinstance(i, int) or i > 0:
                        hold(act, "act", d_out[k], i * 16)
                    normalise(CN, k, P, xin[k], xout[k], d_done)
            dense(0)
            with act.Fori(1, CHUNKS // RINGD) as i:
                dense(i)
            act.wait_ge(d_var, CHUNKS + 1)
            root(1, 0, TAIL, d_sd)
            act.wait_ge(d_scale, CHUNKS + 1)
            act.wait_ge(d_out[0], 16 * (CHUNKS // RINGD))
            normalise(1, 0, TAIL, xin[0], xout[0], d_done)

            def edges(i):
                for h in range(2):
                    g = 2 * i + h
                    hold(act, "act", e_made, g - 1)
                    act.activation(ringA[:, h, :], group(big, g), ACT.Relu, bias=bn[:, 7:8],
                                   scale=bn[:, 5:6]).then_inc(e_relu, 1)
                    hold(act, "act", e_var, g + 1)
                    root(U, h, P, e_sd)
                    hold(act, "act", e_scale, g + 1)
                    hold(act, "act", e_out[h], i * 16 * U)
                    normalise(U, h, P, rows[:, h, :], rows[:, h, :], e_done)
            edges(0)
            with act.Fori(1, PAIRS) as i:
                edges(i)

        @block.vector
        def _(dve):
            step = Steps(dve, "dve", dve_step)

            def two(view, w):
                return view.rearrange("p (n two s) -> p n two s", two=2, s=w)

            def exchange(a, b, w):
                ia, ib = two(a, w), two(b, w)
                step.settle()
                step(dve.tensor_tensor(ib[:, :, 0, :], ia[:, :, 0, :], ia[:, :, 1, :], ALU.min))
                step(dve.tensor_tensor(ib[:, :, 1, :], ia[:, :, 0, :], ia[:, :, 1, :], ALU.max))
                return b, a

            def mirror(a, b, w):
                ia, ib = two(a, w), two(b, w)
                step.settle()
                step(dve.tensor_tensor(ib[:, :, 0, :], ia[:, :, 0, :], ia[:, :, 1, ::-1], ALU.min))
                step(dve.tensor_tensor(ib[:, :, 1, :], ia[:, :, 0, ::-1], ia[:, :, 1, :], ALU.max))
                return b, a

            def sign(a, b, col):
                step.settle()
                step(dve.tensor_scalar(b, a, signs[:, col:col + 1], None, ALU.mult))
                return b, a

            def sort(a, b):
                a, b = sign(a, b, 0)
                for k in range(1, 9):
                    a, b = mirror(a, b, 2 ** (k - 1))
                    for j in range(k - 2, -1, -1):
                        a, b = exchange(a, b, 2 ** j)
                for k in range(9, 16):
                    step.settle()
                    step(dve.transpose(b, a))
                    a, b = b, a
                    if k < 14:
                        step.settle()
                        step(dve.tensor_tensor(b, a, turn[:, k - 9, :], ALU.mult))
                        a, b = b, a
                    if k == 13:
                        a, b = sign(a, b, 1)
                    if k == 14:
                        a, b = sign(a, b, 3)
                    if k == 15:
                        a, b = sign(a, b, 2)
                    for j in range(k - 1, 12, -1):
                        step.settle()
                        for q in range(4):
                            o = q ^ (1 << (j - 13))
                            s = -1.0 if (q >> (j - 13)) & 1 else 1.0
                            step(dve.tensor_scalar(b[32 * q:32 * q + 32, :], a[32 * o:32 * o + 32, :], s, None,
                                                   ALU.mult))
                        step.settle()
                        step(dve.scalar_tensor_tensor(t1, a, signs[:, j - 12:j - 11], b, ALU.mult, ALU.min))
                        step.settle()
                        step(dve.tensor_scalar(b, t1, signs[:, j - 12:j - 11], None, ALU.mult))
                        a, b = b, a
                    for j in range(min(k - 1, 12), 7, -1):
                        a, b = exchange(a, b, 2 ** (j - 8))
                    step.settle()
                    step(dve.transpose(b, a))
                    a, b = b, a
                    for j in range(7, -1, -1):
                        a, b = exchange(a, b, 2 ** j)
                step.settle()
                return a

            def high(values, place_, tmp1, tmp2, out):
                step.settle()
                step(dve.tensor_scalar(tmp1, values, float(HALF), None, ALU.is_ge))
                step(dve.tensor_scalar(tmp2, values, 2.0, -float(2 * HALF + 32767), ALU.mult, ALU.add))
                step.settle()
                step(dve.tensor_tensor(tmp1, tmp1, tmp2, ALU.mult))
                step.settle()
                step(dve.tensor_scalar(tmp2, values, -1.0, float(HALF + 32895), ALU.mult, ALU.add))
                step.settle()
                step(dve.tensor_tensor(out, tmp1, tmp2, ALU.add))

            def unpack(v):
                lo, hi = v.bitcast(U16)[:, 0::2], v.bitcast(U16)[:, 1::2]
                step(dve.tensor_copy(pay, lo))
                step(dve.tensor_scalar(t1, hi, 32768.0, None, ALU.is_ge))
                step(dve.tensor_scalar(t2, hi, -2.0, float(2 * HALF + 32895 - HALF + 128 - HALF), ALU.mult, ALU.add))
                step(dve.tensor_scalar(key, hi, float(HALF - 128), None, ALU.add))
                step.settle()
                step(dve.tensor_tensor(t1, t1, t2, ALU.mult))
                step.settle()
                step(dve.tensor_tensor(key, key, t1, ALU.add))
                step.settle()
                step(dve.tensor_scalar(key1, key, 1.0, None, ALU.add))
                step.settle()

            def mark(same, n):
                dve.sem_inc(sorted_keys, 1)
                step(dve.tensor_tensor(same[:, 1:SORT], key1[:, 1:SORT], key1[:, 0:SORT - 1], ALU.is_equal))
                dve.wait_ge(shifted, 2 * n + 1)
                step(dve.tensor_tensor(same[:, 0:1], key1[:, 0:1], PS[0][:, 0:1], ALU.is_equal))
                step.settle()
                dve.sem_inc(marks, 1)
                dve.wait_ge(shifted, 2 * n + 2)
                rows_ = P if n == 0 else SR
                step(dve.tensor_copy(same[0:rows_, SORT:SORT + 1], PS[0][0:rows_, 2:3]))
                step.settle()

            dve.wait_ge(consts, 1)
            dve.wait_ge(lists_in, 32)
            step(dve.tensor_scalar(sign_i[:, 1:2], sign_i[:, 0:1], 1, None, ALU.bitwise_and))
            step.settle()
            step(dve.tensor_scalar(signs[:, 0:1], sign_i[:, 1:2], -2.0, 1.0, ALU.mult, ALU.add))
            lo, hi = va.bitcast(U16)[:, 0::2], va.bitcast(U16)[:, 1::2]
            step(dve.memset(hi, HALF + 128))
            step(dve.memset(lo, N))
            high(raw[0:LP, 0:LC], None, t1[0:LP, 0:LC], t2[0:LP, 0:LC], hi[0:LP, 0:LC])
            step(dve.tensor_copy(lo[0:LP, 0:LC], raw[0:LP, LC:2 * LC]))
            v = sort(va, vb)
            unpack(v)
            mark(same1, 0)
            step(dve.tensor_copy(same16, same1[:, 0:SORT]))
            step(dve.scalar_tensor_tensor(t2, same1[:, 1:SORT + 1], float(SKIP), key, ALU.mult, ALU.add))
            step.settle()
            dve.sem_inc(marks, 1)
            dve.wait_ge(turned, 1)
            for m, (dest, top) in enumerate(((dst_i, N - 1.0), (src_i, N - 1.0), (out_i, 2.0 * SKIP))):
                psv = PS[m][:, 0:2 * P].rearrange("p (c t) -> p c t", c=2)[:, :, 0:SR]
                step(dve.tensor_scalar(dest[:, :].rearrange("p (t c) -> p c t", c=2), psv, top, None, ALU.min))
            step.settle()
            dve.sem_inc(indexed, 1)

            step(dve.tensor_copy(t1, place[:, :].bitcast(I32)))
            step.settle()
            step(dve.tensor_copy(key, pay))
            step(dve.tensor_scalar(t2[:, 0:1], sign_i[:, 0:1], float(SR), None, ALU.is_ge))
            step.settle()
            step(dve.tensor_scalar(t2[:, 0:1], t2[:, 0:1], float(ROWS), None, ALU.mult))
            step.settle()
            v0 = va if v is vb else vb
            other = v
            lo, hi = v0.bitcast(U16)[:, 0::2], v0.bitcast(U16)[:, 1::2]
            step(dve.tensor_scalar(lo, t1, t2[:, 0:1], None, ALU.add))
            step.settle()
            high(key, None, t1, t2, hi)
            v = sort(v0, other)
            unpack(v)
            mark(same2, 1)
            dve.sem_inc(marks, 1)
            dve.wait_ge(turned, 2)
            psv = PS[1][:, 0:2 * P].rearrange("p (c t) -> p c t", c=2)[:, :, 0:SR]
            step(dve.tensor_scalar(row_i[:, :].rearrange("p (t c) -> p c t", c=2), psv, ROWS - 1.0, None, ALU.min))
            step.settle()
            dve.sem_inc(indexed, 1)

            def scores(i):
                for h in range(2):
                    g = 2 * i + h
                    hold(dve, "dve", q_made, g + 1)
                    hold(dve, "dve", s_made, g - 1)
                    dve.scalar_tensor_tensor(ringB[:, h, :], PS[1][:, 0:GW], bqc[:, 0:1], group(big, g),
                                             ALU.add, ALU.mult).then_inc(qk_ready, 1)
                    hold(dve, "dve", m_made, g + 1)
                    hold(dve, "dve", qk_ready, g + 1)
                    dve.tensor_tensor(group(big, g).rearrange("p (n d) -> p n d", d=D),
                                      PS[2][:, 0:GW].rearrange("p (n d) -> p n d", d=D),
                                      bmr[:, :].unsqueeze(1).to_broadcast([P, U, D]), ALU.add).then_inc(m_kept, 1)
                    hold(dve, "dve", s_made, g + 1)
                    dve.tensor_copy(sc[:, bass.ds(g * U * H, U * H)], PS[3][:, 0:U * H]).then_inc(s_kept, 1)
            dve.wait_ge(k_kept, GROUPS)
            dve.wait_ge(biases_in, 16 * 7)
            scores(0)
            with dve.Fori(1, PAIRS) as i:
                scores(i)

            def take_scores(i):
                for h in range(2):
                    g = 2 * i + h
                    hold(dve, "dve", g_in[h], (i + 1) * 16 * U)
                    dve.tensor_copy(gs[:, :, bass.ds(g * U, U)],
                                    small[:, h, :].rearrange("p (t h) -> p h t", h=H)).then_inc(g_kept, 1)
            take_scores(0)
            with dve.Fori(1, PAIRS) as i:
                take_scores(i)
            sp_, sn_ = same2[0:SR, 0:SORT], same2[0:SR, 1:SORT + 1]
            K = H + 1
            segs = [seg[0:SR, j * SORT:(j + 1) * SORT] for j in range(K)]
            fwds = [fwd[0:SR, j * SORT:(j + 1) * SORT] for j in range(K)]
            bwds = [bwd[0:SR, j * SORT:(j + 1) * SORT] for j in range(K)]
            ng = negs[0:SR, :]
            step(dve.tensor_scalar(ng, sp_, 1.0, -LOW, ALU.subtract, ALU.mult))
            step(dve.memset(segs[H], 1.0))
            step(dve.tensor_reduce(pack[0:SR, 10:11], sp_, AX.X, ALU.min))
            step(dve.tensor_reduce(pack[0:SR, 11:12], sn_, AX.X, ALU.min))
            dve.wait_ge(soft_dve, 1)
            step(dve.tensor_copy(seg[0:SR, 0:H * SORT], PS[0][0:SR, 0:H * SORT]))
            step.settle()
            turn_no = [1]

            def cross(count, back, last, whole, start, op0, op1):
                step.settle()
                for j in range(count):
                    step(dve.tensor_copy(pack[0:SR, j:j + 1], last(j)))
                    step(dve.tensor_copy(pack[0:SR, K + j:K + j + 1], whole))
                step.settle()
                dve.sem_inc(soft_pe, 1)
                turn_no[0] += 1
                dve.wait_ge(soft_dve, turn_no[0])
                step(dve.tensor_copy(crow[0:count, :].rearrange("p (a n) -> p a n", a=2)[:, :, 0:SR],
                                     PS[3][0:count, 0:2 * P].rearrange("p (a n) -> p a n", a=2)[:, :, 0:SR]))
                step(dve.memset(cscan[0:count, :], start))
                step.settle()
                a, b = crow[0:count, P:P + SR], crow[0:count, 0:SR]
                if back:
                    step(dve.tensor_tensor_scan(cscan[0:count, 0:SR][:, ::-1], a[:, ::-1], b[:, ::-1], start, op0, op1))
                else:
                    step(dve.tensor_tensor_scan(cscan[0:count, 1:SR + 1], a, b, start, op0, op1))
                step.settle()
                dve.sem_inc(soft_pe, 1)
                turn_no[0] += 1
                dve.wait_ge(soft_dve, turn_no[0])
                step(dve.tensor_copy(carry[0:SR, 0:count], PS[3][0:SR, 512:512 + count]))
                step.settle()

            def forward(count, data, mask, start, op0, op1, whole):
                step.settle()
                for j in range(count):
                    step(dve.tensor_tensor_scan(fwds[j], mask, data[j], start, op0, op1))
                cross(count, False, lambda j: fwds[j][:, SORT - 1:SORT], whole, start, op0, op1)
                for j in range(count):
                    step(dve.tensor_tensor_scan(fwds[j], mask, data[j], carry[0:SR, j:j + 1], op0, op1))
                step.settle()

            def backward(count, whole):
                for j in range(count):
                    step(dve.scalar_tensor_tensor(fwds[j], sn_, 0.0, fwds[j], ALU.is_equal, ALU.mult))
                step.settle()
                for j in range(count):
                    step(dve.tensor_tensor_scan(bwds[j][:, ::-1], sn_[:, ::-1], fwds[j][:, ::-1], 0.0,
                                                ALU.mult, ALU.add))
                cross(count, True, lambda j: bwds[j][:, 0:1], whole, 0.0, ALU.mult, ALU.add)
                for j in range(count):
                    step(dve.tensor_tensor_scan(bwds[j][:, ::-1], sn_[:, ::-1], fwds[j][:, ::-1],
                                                carry[0:SR, j:j + 1], ALU.mult, ALU.add))
                step.settle()

            step(dve.tensor_scalar(pack[0:SR, 10:11], pack[0:SR, 10:11], 1.0, None, ALU.mult))
            step.settle()
            step(dve.tensor_scalar(t1[0:SR, 0:1], pack[0:SR, 10:11], 1.0, -LOW, ALU.subtract, ALU.mult))
            step.settle()
            forward(H, segs, ng, LOW, ALU.add, ALU.max, t1[0:SR, 0:1])
            backward(H, pack[0:SR, 11:12])
            step(dve.tensor_tensor(bwd[0:SR, 0:H * SORT], seg[0:SR, 0:H * SORT], bwd[0:SR, 0:H * SORT], ALU.subtract))
            step.settle()
            dve.sem_inc(soft_act, 1)
            dve.wait_ge(soft_exp, 1)
            forward(K, segs, sp_, 0.0, ALU.mult, ALU.add, pack[0:SR, 10:11])
            backward(K, pack[0:SR, 11:12])
            for j in range(H):
                step(dve.reciprocal(fwds[j], bwds[j]))
                step(dve.tensor_tensor(segs[j], segs[j], bwds[H], ALU.mult))
            step.settle()
            for j in range(H):
                step(dve.tensor_tensor(segs[j], segs[j], fwds[j], ALU.mult))
            step.settle()
            dve.sem_inc(soft_pe, 1)
            turn_no[0] += 1
            dve.wait_ge(soft_dve, turn_no[0])
            gsv = gs[:, :, :].rearrange("p h t -> p (h t)").rearrange("p (t c h) -> p c h t", c=2, h=H)
            psw = PS[1][:, :].rearrange("p (h c t) -> p c h t", h=H, c=2)
            for c in range(2):
                step(dve.tensor_copy(gsv[:, c, :, :], psw[:, c, :, 0:SR]))
            step.settle()
            dve.sem_inc(weights_ready, 2)

            dve.wait_ge(alpha_in, 16)

            def weigh(g, h):
                hold(dve, "dve", o_turned, g - 1)
                dve.tensor_tensor(ringA[:, h, :].rearrange("p (n d) -> p n d", d=DH),
                                  group(big, g).rearrange("p (n d) -> p n d", d=DH),
                                  sc[:, bass.ds(g * U * H, U * H)].unsqueeze(2).to_broadcast([P, U * H, DH]),
                                  ALU.mult).then_inc(o_made, 1)

            def scan(g, h, i):
                hold(dve, "dve", o_turned, g + 1)
                hold(dve, "dve", f_in[h], i * 16)
                hold(dve, "dve", h_made, g - 1)
                hold(dve, "dve", run_sums, g)
                first = isinstance(g, int) and g == 0
                dve.tensor_tensor_scan(ringB[:, h, :], flags[:, h, 0:GW], PS[0][:, 0:GW],
                                       0.0 if first else ringB[:, 1 - h, GW - 1:GW],
                                       ALU.mult, ALU.add).then_inc(run_sums, 1)

            def keep(g, h):
                hold(dve, "dve", h_made, g + 1)
                dve.scalar_tensor_tensor(group(big, g), flags[:, h, 1:GW + 1], 0.0, PS[1][:, 0:GW],
                                         ALU.is_equal, ALU.mult,
                                         accum_out=sums[:, 0, bass.ds(g, 1)]).then_inc(h_kept, 1)

            weigh(0, 0)
            weigh(1, 1)
            scan(0, 0, 1)
            with dve.Fori(1, PAIRS) as i:
                for h in range(2):
                    g = 2 * i + h
                    weigh(g, h)
                    scan(g - 1, 1 - h, i + h)
                    keep(g - 2, h)
            scan(GROUPS - 1, 1, PAIRS)
            keep(GROUPS - 2, 0)
            keep(GROUPS - 1, 1)

            dve.wait_ge(squares, 1)
            dve.wait_ge(h_kept, GROUPS)
            step(dve.tensor_reduce(bn[:, 0:2], sums[:, :, :], AX.X, ALU.add))
            step.settle()
            step(dve.tensor_scalar(bn[:, 0:2], bn[:, 0:2], 1.0 / N, None, ALU.mult))
            step.settle()
            step(dve.tensor_tensor(bn[:, 4:5], bn[:, 0:1], bn[:, 0:1], ALU.mult))
            step(dve.tensor_tensor(bn[:, 6:7], bn[:, 0:1], b1c[:, 0:1], ALU.add))
            step.settle()
            step(dve.tensor_tensor(bn[:, 2:3], bn[:, 1:2], bn[:, 4:5], ALU.subtract))
            step.settle()
            dve.sem_inc(bn_var, 1)
            dve.wait_ge(bn_sd, 1)
            step(dve.reciprocal(bn[:, 4:5], bn[:, 3:4]))
            step(dve.tensor_tensor(bn[:, 6:7], b1c[:, 0:1], bn[:, 6:7], ALU.subtract))
            step.settle()
            step(dve.tensor_tensor(bn[:, 5:6], bn[:, 4:5], gammac[:, 0:1], ALU.mult))
            step.settle()
            step(dve.scalar_tensor_tensor(bn[:, 7:8], bn[:, 6:7], bn[:, 5:6], betac[:, 0:1], ALU.mult, ALU.add))
            step.settle()
            dve.sem_inc(bn_bias, 1)
            dve.wait_ge(rest_made, 1)
            step(dve.tensor_tensor(rest[:, :], PS[2][:, 0:D], b2r[:, :], ALU.add))
            step.settle()
            dve.sem_inc(rest_ready, 1)

            def moments(n, k, p, data, var):
                s = lnst[0:p, k, 0:6 * n].rearrange("p (n s) -> p n s", s=6)
                q = lnsm[0:p, k]
                for j in range(n):
                    step(dve.bn_stats(lnst[0:p, k, 6 * j:6 * j + 6], data[0:p, j * D:(j + 1) * D]))
                step.settle()
                step(dve.tensor_tensor(q[:, 0, 0:n], s[:, :, 1], s[:, :, 4], ALU.add))
                step(dve.tensor_tensor(q[:, 1, 0:n], s[:, :, 1], s[:, :, 4], ALU.subtract))
                step(dve.tensor_tensor(q[:, 2, 0:n], s[:, :, 2], s[:, :, 5], ALU.add))
                step.settle()
                step(dve.tensor_tensor(q[:, 1, 0:n], q[:, 1, 0:n], q[:, 1, 0:n], ALU.mult))
                step.settle()
                dve.scalar_tensor_tensor(q[:, 3, 0:n], q[:, 1, 0:n], D / 4.0, q[:, 2, 0:n],
                                         ALU.mult, ALU.add).then_inc(var, 1)

            def factors(n, k, p, ready):
                q = lnsm[0:p, k]
                step(dve.reciprocal(q[:, 5, 0:n], q[:, 4, 0:n]))
                step.settle()
                dve.scalar_tensor_tensor(q[:, 6, 0:n], q[:, 0, 0:n], -0.5, q[:, 5, 0:n],
                                         ALU.mult, ALU.mult).then_inc(ready, 1)

            def dense(i):
                for k in range(RINGD):
                    c = RINGD * i + k
                    hold(dve, "dve", d_added, c + 1)
                    hold(dve, "dve", d_done, c - RINGD + 1)
                    moments(CN, k, P, xin[k], d_var)
                    hold(dve, "dve", d_sd, c + 1)
                    factors(CN, k, P, d_scale)
            step.loop(dve, 0, CHUNKS // RINGD, dense)
            dve.wait_ge(d_added, CHUNKS + 1)
            dve.wait_ge(d_done, CHUNKS)
            moments(1, 0, TAIL, xin[0], d_var)
            dve.wait_ge(d_sd, CHUNKS + 1)
            factors(1, 0, TAIL, d_scale)
            dve.wait_ge(d_done, CHUNKS + 1)

            def edges(i):
                for h in range(2):
                    g = 2 * i + h
                    hold(dve, "dve", e_in[h], (i + 1) * 16)
                    hold(dve, "dve", e_out[h], i * 16 * U)
                    step(dve.tensor_tensor(rows[:, h, :].rearrange("p (n d) -> p n d", d=D),
                                           ringB[:, h, :].rearrange("p (n d) -> p n d", d=D),
                                           b2r[:, :].unsqueeze(1).to_broadcast([P, U, D]), ALU.add))
                    step.settle()
                    hold(dve, "dve", e_made, g + 1)
                    dve.tensor_tensor(rows[:, h, :], rows[:, h, :], PS[h][:, 0:GW], ALU.add).then_inc(e_read, 1)
                    hold(dve, "dve", e_read, g + 1)
                    hold(dve, "dve", e_done, g - 1)
                    moments(U, h, P, rows[:, h, :], e_var)
                    hold(dve, "dve", e_sd, g + 1)
                    factors(U, h, P, e_scale)
            step.loop(dve, 0, PAIRS, edges)

        @block.tensor
        def _(pe):
            pe.wait_ge(consts, 1)

            def wide(out, w, data):
                pe.matmul(out[:, 0:512], w[:, :], data[:, 0:512], start=True, stop=True)
                return pe.matmul(out[:, 512:GW], w[:, :], data[:, 512:GW], start=True, stop=True)

            def flip(out, data):
                for k in range(U):
                    last = pe.transpose(out[:, k * P:(k + 1) * P], data[:, k * P:(k + 1) * P], ident[:, :])
                return last

            def after_sort(n):
                pe.wait_ge(sorted_keys, n + 1)
                if n:
                    pe.wait_ge(kx_ready, GROUPS)
                    pe.wait_ge(k_kept, GROUPS)
                pe.matmul(PS[0][:, 0:1], down[:, :], key1[:, SORT - 1:SORT], start=True, stop=True).then_inc(shifted, 1)
                pe.wait_ge(marks, 2 * n + 1)
                same, r = (same1, P) if n == 0 else (same2, SR)
                pe.matmul(PS[0][0:r, 2:3], up[0:r, 0:r], same[0:r, 0:1], start=True, stop=True).then_inc(shifted, 1)
                pe.wait_ge(marks, 2 * n + 2)
                for m, t in enumerate((key, pay, t2) if n == 0 else (key, pay)):
                    for c in range(2):
                        last = pe.transpose(PS[m][:, c * P:(c + 1) * P], t[:, c * P:(c + 1) * P], ident[:, :])
                last.then_inc(turned, 1)

            after_sort(0)
            pe.wait_ge(indexed, 1)
            pe.wait_ge(weights_in, 16 * 5)

            def keys(i):
                for h in range(2):
                    g = 2 * i + h
                    hold(pe, "pe", kd_in[h], (i + 1) * 16 * U)
                    hold(pe, "pe", kx_ready, g)
                    flip(PS[0], rows[:, h, :]).then_inc(kd_turned, 1)
                    hold(pe, "pe", kx_ready, g + 1)
                    hold(pe, "pe", k_kept, g)
                    wide(PS[1], wk, ringA[:, h, :]).then_inc(k_made, 1)
            keys(0)
            with pe.Fori(1, PAIRS) as i:
                keys(i)
            after_sort(1)
            pe.wait_ge(indexed, 2)

            def scores(i):
                for h in range(2):
                    g = 2 * i + h
                    hold(pe, "pe", qs_in[h], (i + 1) * 16 * U)
                    hold(pe, "pe", qx_ready, g)
                    flip(PS[0], rows[:, h, :]).then_inc(qs_turned, 1)
                    hold(pe, "pe", qx_ready, g + 1)
                    hold(pe, "pe", qk_ready, g)
                    wide(PS[1], wq, ringA[:, h, :]).then_inc(q_made, 1)
                    hold(pe, "pe", m_kept, g)
                    for k in range(U):
                        last = pe.matmul(PS[2][:, k * D:(k + 1) * D], ringA[:, h, k * P:(k + 1) * P], wm[:, :],
                                         start=True, stop=True)
                    last.then_inc(m_made, 1)
                    hold(pe, "pe", qk_ready, g + 1)
                    hold(pe, "pe", s_kept, g)
                    for k in range(U):
                        last = pe.matmul(PS[3][:, k * H:(k + 1) * H], ringB[:, h, k * P:(k + 1) * P], heads[:, :],
                                         start=True, stop=True)
                    last.then_inc(s_made, 1)
            scores(0)
            with pe.Fori(1, PAIRS) as i:
                scores(i)

            pe.wait_ge(g_kept, GROUPS)
            for h in range(H):
                for c in range(2):
                    last = pe.transpose(PS[0][0:SR, (2 * h + c) * P:(2 * h + c + 1) * P],
                                        gs[:, h, :].rearrange("p (t c) -> p c t", c=2)[:, c, :], ident[:, :])
            last.then_inc(soft_dve, 1)
            asked = 0
            for count in (H, H, H + 1, H + 1):
                asked += 1
                pe.wait_ge(soft_pe, asked)
                pe.transpose(PS[3][0:count, 0:SR], pack[0:SR, 0:count], ident[0:SR, 0:SR])
                pe.transpose(PS[3][0:count, P:P + SR], pack[0:SR, H + 1:H + 1 + count],
                             ident[0:SR, 0:SR]).then_inc(soft_dve, 1)
                asked += 1
                pe.wait_ge(soft_pe, asked)
                at = 1 if asked in (4, 8) else 0
                pe.transpose(PS[3][0:SR, 512:512 + count], cscan[0:count, at:at + SR],
                             ident[0:count, 0:count]).then_inc(soft_dve, 1)
            pe.wait_ge(soft_pe, asked + 1)
            for h in range(H):
                for c in range(2):
                    last = pe.transpose(PS[1][:, (2 * h + c) * P:(2 * h + c) * P + SR],
                                        seg[0:SR, h * SORT + c * P:h * SORT + (c + 1) * P], ident[0:SR, 0:SR])
            last.then_inc(soft_dve, 1)
            pe.wait_ge(weights_ready, 1)

            def flip_sums(g, h):
                hold(pe, "pe", o_made, g + 1)
                hold(pe, "pe", run_sums, g)
                flip(PS[0], ringA[:, h, :]).then_inc(o_turned, 1)

            def first_layer(g, h):
                hold(pe, "pe", run_sums, g + 1)
                hold(pe, "pe", h_kept, g)
                wide(PS[1], w1, ringB[:, h, :]).then_inc(h_made, 1)

            flip_sums(0, 0)
            flip_sums(1, 1)
            first_layer(0, 0)
            with pe.Fori(1, PAIRS) as i:
                for h in range(2):
                    g = 2 * i + h
                    flip_sums(g, h)
                    first_layer(g - 1, 1 - h)
            first_layer(GROUPS - 1, 1)

            pe.wait_ge(bn_rest, 1)
            pe.matmul(PS[2][:, 0:D], bn[:, 8:9].to_broadcast([P, P]), w2[:, :], start=True, stop=True)\
              .then_inc(rest_made, 1)

            def edges(i):
                for h in range(2):
                    g = 2 * i + h
                    hold(pe, "pe", e_relu, g + 1)
                    hold(pe, "pe", e_read, g - 1)
                    for k in range(U):
                        last = pe.matmul(PS[h][:, k * D:(k + 1) * D], ringA[:, h, k * P:(k + 1) * P], w2[:, :],
                                         start=True, stop=True)
                    last.then_inc(e_made, 1)
            edges(0)
            with pe.Fori(1, PAIRS) as i:
                edges(i)


_NAMES = ["x", "src", "dst", "L0_gnn_Wk", "L0_gnn_bk", "L0_gnn_Wm", "L0_gnn_bm", "L0_gnn_Wq", "L0_gnn_bq",
          "L0_gnn_W1", "L0_gnn_b1", "L0_gnn_gamma", "L0_gnn_beta", "L0_gnn_W2", "L0_gnn_b2"]


def kernel(**inputs):
    import numpy as np
    import concourse.bacc as bacc
    from concourse.bass_utils import run_bass_kernel_spmd as run

    nc = bacc.Bacc("TRN2", target_bir_lowering=False, num_devices=1)
    arrays, args = {}, []
    for name in _NAMES:
        a = np.ascontiguousarray(inputs[name])
        arrays[f"in_{name}"] = a
        args.append(nc.dram_tensor(f"in_{name}", a.shape, mybir.dt.from_np(a.dtype), kind="ExternalInput").ap())
    y = nc.dram_tensor("y", (N, D), F32, kind="ExternalOutput").ap()
    build(nc, *args, y)
    return run(nc, [arrays], core_ids=[0]).results[0]["y"]
```

```python
import math
from contextlib import ExitStack

import concourse.bass as bass
from concourse import mybir

F32 = mybir.dt.float32
BF16 = mybir.dt.bfloat16
I32 = mybir.dt.int32
U16 = mybir.dt.uint16
ALU = mybir.AluOpType
ACT = mybir.ActivationFunctionType
AX = mybir.AxisListType

N = 50000
E = 25000
D = 128
H = 4
DH = D // H
EPS = 1e-5
P = 128
TILES = -(-E // P)
U = 7
GROUPS = TILES // U
PAIRS = GROUPS // 2
QUADS = GROUPS // 4
GW = U * P
ROWS = TILES * P
SORT = 256
SR = TILES // 2
LP = E // SORT
CN = 14
CHUNK = P * CN
CHUNKS = -(-N // CHUNK)
CW = CN * D
LAG = 3
CA = 11
REACH = (N - CHUNK) // (CHUNKS - 1)
ROOM = 9984
LOW = -1.0e30
SKIP = 100000
HALF = N // 2

assert CHUNKS == GROUPS


def build(nc, x, src, dst, Wk, bk, Wm, bm, Wq, bq, W1, b1, gamma, beta, W2, b2, y, DEBUG=None):
    ctx = ExitStack()
    with ctx:
        def sb(name, shape, dt=F32):
            return ctx.enter_context(nc.sbuf_tensor(name, shape, dt))

        def sem(name):
            return ctx.enter_context(nc.semaphore(name))

        xdst_d = nc.dram_tensor("xdst_d", [GROUPS, P, GW], F32).ap()
        scores_d = nc.dram_tensor("scores_d", [ROWS, H], F32).ap()
        alpha_d = nc.dram_tensor("alpha_d", [ROWS, H], F32).ap()
        back_d = nc.dram_tensor("back_d", [P * SORT], I32).ap()
        same_d = nc.dram_tensor("same_d", [P * SORT], BF16).ap()

        ident = sb("ident", [P, P])
        down = sb("down", [P, P])
        up = sb("up", [P, P])
        heads = sb("heads", [P, H])
        wk, wq, wm, w1, w2 = (sb(n, [P, D]) for n in ("wk", "wq", "wm", "w1", "w2"))
        bkc, bqc, b1c, b2c, gammac, betac = (sb(n, [P, 1]) for n in ("bkc", "bqc", "b1c", "b2c", "gammac", "betac"))
        bmr = sb("bmr", [P, D])
        b2r = sb("b2r", [P, D])
        epsc = sb("epsc", [P, 1])
        sign_i = sb("sign_i", [P, 2], I32)
        signs = sb("signs", [P, 6])
        turn = sb("turn", [P, 5, SORT])
        place = sb("place", [P, SORT])

        big = sb("big", [P, ROWS])
        dst_i = sb("dst_i", [P, TILES + U], I32)
        src_i = sb("src_i", [P, TILES + U], I32)
        out_i = sb("out_i", [P, TILES + U], I32)
        row_i = sb("row_i", [P, TILES + U], I32)
        back_i = sb("back_i", [P, TILES + U], I32)
        stage = sb("stage", [P, 4, U], I32)
        rows = sb("rows", [P, 2, GW])
        ringA = sb("ringA", [P, 2, GW])
        ringB = sb("ringB", [P, 2, GW])
        zring = sb("zring", [P, 4, GW])
        flags = sb("flags", [P, 4, GW + 2], BF16)
        small = sb("small", [P, 2, U * H])
        sc = sb("sc", [P, TILES * H])
        gs = sb("gs", [P, H, TILES])
        sums = sb("sums", [P, 2, GROUPS])
        bn = sb("bn", [P, 12])
        rest = sb("rest", [P, D])
        late_i = sb("late_i", [1, 1], I32)
        lnst = sb("lnst", [P, 8, CN * 6])
        lnsm = sb("lnsm", [P, 8, 8, CN])

        room = sb("room", [P, ROOM])
        used = [0]

        def take(n):
            used[0] += n
            assert used[0] <= ROOM
            return room[:, used[0] - n:used[0]]

        va, vb, t1, t2 = (take(SORT) for _ in range(4))
        key, pay, key1 = (take(SORT) for _ in range(3))
        same1 = take(SORT + 1)
        same2 = take(SORT + 1)
        later = take(SORT)
        seqno = take(SORT).bitcast(I32)
        way = take(SORT).bitcast(I32)
        same16 = take(SORT // 2).bitcast(BF16)
        raw = take(2 * SORT).bitcast(I32)
        one_i = take(2).bitcast(I32)
        seg = take((H + 1) * SORT)
        fwd = take((H + 1) * SORT)
        bwd = take((H + 1) * SORT)
        negs = take(SORT)
        pack = take(12)
        crow = take(2 * P)
        cscan = take(P + 2)
        carry = take(8)
        xin = [room[:, i * CW:(i + 1) * CW] for i in range(4)]
        final_rows = [rows[:, 0], rows[:, 1], ringB[:, 0], ringB[:, 1]]
        bound = sc[:, 0:TILES]
        ends = sc[:, TILES:2 * TILES]
        counted = sc[:, 2 * TILES:2 * TILES + 1]

        PS = [ctx.enter_context(nc.psum_tensor(f"ps{i}", [P, 1024], F32)) for i in range(4)]

        pace = {n: sem(f"pace_{n}") for n in ("sp", "pool", "act", "dve", "pe")}
        lists_in, weights_in, biases_in = sem("lists_in"), sem("weights_in"), sem("biases_in")
        consts = sem("consts")
        raw_clear = sem("raw_clear")
        order_pe = sem("order_pe")
        order_dve = sem("order_dve")
        dve_step, act_step, pe_step, pool_step = sem("dve_step"), sem("act_step"), sem("pe_step"), sem("pool_step")
        sorted_keys = sem("sorted_keys")
        shifted = sem("shifted")
        marks = sem("marks")
        turned = sem("turned")
        indexed = sem("indexed")
        marks_out = sem("marks_out")
        kd_in = [sem(f"kd_in{h}") for h in range(2)]
        kd_saved = [sem(f"kd_saved{h}") for h in range(2)]
        kd_turned = sem("kd_turned")
        kx_ready = sem("kx_ready")
        k_made = sem("k_made")
        k_kept = sem("k_kept")
        qs_in = [sem(f"qs_in{h}") for h in range(2)]
        qs_turned = sem("qs_turned")
        qx_ready = sem("qx_ready")
        q_made = sem("q_made")
        qk_ready = sem("qk_ready")
        m_made = sem("m_made")
        m_kept = sem("m_kept")
        s_made = sem("s_made")
        s_kept = sem("s_kept")
        scores_out = sem("scores_out")
        g_in = [sem(f"g_in{h}") for h in range(2)]
        g_kept = sem("g_kept")
        soft_pe = sem("soft_pe")
        soft_dve = sem("soft_dve")
        soft_act = sem("soft_act")
        soft_exp = sem("soft_exp")
        weights_ready = sem("weights_ready")
        way_ready = sem("way_ready")
        back_out, back_in = sem("back_out"), sem("back_in")
        alpha_out = sem("alpha_out")
        a_in = [sem(f"a_in{h}") for h in range(2)]
        f_in = [sem(f"f_in{h}") for h in range(4)]
        o_made = sem("o_made")
        o_turned = sem("o_turned")
        run_sums = sem("run_sums")
        h_made = sem("h_made")
        h_kept = sem("h_kept")
        squares = sem("squares")
        bn_var = sem("bn_var")
        bn_sd = sem("bn_sd")
        bn_bias = sem("bn_bias")
        bn_rest = sem("bn_rest")
        rest_made = sem("rest_made")
        rest_ready = sem("rest_ready")
        d_in = [sem(f"d_in{i}") for i in range(4)]
        d_out = [sem(f"d_out{i}") for i in range(4)]
        d_var, d_sd, d_scale, d_done = (sem(f"d_{n}") for n in ("var", "sd", "scale", "done"))
        d_part = sem("d_part")
        late_ready = sem("late_ready")
        late_pe, late_dve = sem("late_pe"), sem("late_dve")
        kb_kept = sem("kb_kept")
        e_in = [sem(f"e_in{h}") for h in range(4)]
        e_relu, e_made, e_var, e_sd, e_scale, e_done = (
            sem(f"e_{n}") for n in ("relu", "made", "var", "sd", "scale", "done"))
        e_out = [sem(f"e_out{h}") for h in range(4)]

        def hold(eng, name, s, value):
            if isinstance(value, int):
                if value > 0:
                    eng.wait_ge(s, value)
            else:
                eng.wait_ge(s, value)
                eng.sem_inc(pace[name], 1)

        class Steps:

            def __init__(self, eng, name, s):
                self.eng, self.name, self.sem, self.n, self.local = eng, name, s, 0, 0

            def __call__(self, ins):
                ins.then_inc(self.sem, 1)
                self.local += 1

            def skip(self, n):
                self.settle()
                self.eng.sem_inc(self.sem, n)
                self.local += n

            def until(self, local):
                hold(self.eng, self.name, self.sem, self.n + local)

            def settle(self):
                hold(self.eng, self.name, self.sem, self.n + self.local)

            def loop(self, eng, first, last, body):
                self.n, self.local = self.n + self.local, 0
                start = self.n
                body(first)
                self.settle()
                once = self.local
                self.local = 0
                with eng.Fori(first + 1, last) as i:
                    self.n = start + once + (i - (first + 1)) * once
                    body(i)
                    self.settle()
                    assert self.local == once, (self.local, once)
                self.n, self.local = start + (last - first) * once, 0

        def group(t, g):
            return t[:, bass.ds(g * GW, GW)]

        block = ctx.enter_context(nc.Block())

        @block.sync
        def _(sp):
            sp.wait_ge(raw_clear, 1)
            for a, edges_ in ((0, dst), (SORT, src)):
                sp.dma_start(raw[0:LP, a:a + SORT],
                             edges_[0:LP * SORT].rearrange("(p n) -> p n", p=LP)).then_inc(lists_in, 16)
                sp.dma_start(raw[LP:LP + 1, a:a + E - LP * SORT],
                             edges_[LP * SORT:E].rearrange("(p n) -> p n", p=1)).then_inc(lists_in, 16)
            for t, w in ((wk, Wk), (wq, Wq), (wm, Wm), (w1, W1), (w2, W2)):
                sp.dma_start(t[:, :], w).then_inc(weights_in, 16)
            for t, b in ((bkc, bk), (bqc, bq), (b1c, b1), (b2c, b2), (gammac, gamma), (betac, beta)):
                sp.dma_start(t[:, :], b.rearrange("(p o) -> p o", o=1)).then_inc(biases_in, 16)
            for t, b in ((bmr, bm), (b2r, b2)):
                sp.dma_start(t[:, :], b.partition_broadcast(P)).then_inc(biases_in, 16)
            sp.wait_ge(indexed, 1)
            sp.dma_start(same_d.rearrange("(p n) -> p n", p=P), same16).then_inc(marks_out, 16)

            def save(i):
                for h in range(2):
                    hold(sp, "sp", kb_kept, 2 * i + h + 1)
                    sp.dma_start(xdst_d[bass.ds(2 * i + h, 1), :, :].rearrange("o p n -> (o p) n"),
                                 ringB[:, h, :]).then_inc(kd_saved[h], 16)
            save(0)
            with sp.Fori(1, PAIRS) as i:
                save(i)

            sp.wait_ge(way_ready, 1)
            sp.dma_start(back_d.rearrange("(p n) -> p n", p=P), way).then_inc(back_out, 16)
            sp.wait_ge(back_out, 16)
            sp.dma_start(back_i[:, 0:TILES], back_d[0:ROWS].rearrange("(p t) -> p t", p=P)).then_inc(back_in, 16)

            sp.wait_ge(s_kept, GROUPS)
            sp.dma_start(scores_d.rearrange("(p t) h -> p (t h)", p=P), sc[:, :]).then_inc(scores_out, 16)

            sp.wait_ge(weights_ready, 1)
            sp.dma_start(alpha_d.rearrange("(p f) h -> p (f h)", p=SR), bwd[0:SR, 0:H * SORT]).then_inc(alpha_out, 16)

            sp.wait_ge(marks_out, 16)

            def load_marks(i):
                for h in range(4):
                    g = 4 * i + h
                    hold(sp, "sp", h_kept, g - 3)
                    sp.dma_start(flags[:, h, 0:GW + 1],
                                 same_d[bass.ds(g * GW, GW + 1)].partition_broadcast(P)).then_inc(f_in[h], 16)
            load_marks(0)
            with sp.Fori(1, QUADS) as i:
                load_marks(i)

            sp.wait_ge(late_ready, 1)
            late = sp.value_load(late_i[0:1, 0:1], min_val=0, max_val=ROWS)
            sp.wait_ge(alpha_out, 16)

            def nodes(t, c):
                first = N - CHUNK if isinstance(c, int) and c == CHUNKS - 1 else c * CHUNK
                return t[bass.ds(first, CHUNK), :].rearrange("(p n) d -> p (n d)", p=P)

            def store(c, k):
                hold(sp, "sp", d_done, c + 1)
                hold(sp, "sp", d_part, c + 1)
                if isinstance(c, int) and c == CHUNKS - 1:
                    sp.wait_ge(d_out[(c - 1) % 4], 16 * QUADS)
                sp.dma_start(nodes(y, c), xin[k]).then_inc(d_out[k], 16)

            def turns(i, dense, edge):
                for h in range(4):
                    s = 4 * i + h
                    if edge:
                        hold(sp, "sp", e_made, s - 3)
                        sp.dma_start(zring[:, h, :],
                                     xdst_d[bass.ds(s, 1), :, :].rearrange("o p n -> (o p) n")).then_inc(e_in[h], 16)
                    if dense:
                        hold(sp, "sp", d_out[h], i * 16)
                        sp.dma_start(xin[h], nodes(x, s)).then_inc(d_in[h], 16)
                        if not isinstance(s, int) or s >= LAG:
                            store(s - LAG, (h - LAG) % 4)

            def work(dense, edge):
                turns(0, dense, edge)
                with sp.Fori(1, QUADS - 1) as i:
                    turns(i, dense, edge)
                turns(QUADS - 1, dense, edge)
                if dense:
                    for c in range(CHUNKS - LAG, CHUNKS):
                        store(c, c % 4)

            with sp.If(late > 0):
                work(True, False)
                work(False, True)
            with sp.Else():
                work(True, True)
            for h in range(4):
                sp.wait_ge(d_out[h], 16 * QUADS)
                sp.wait_ge(e_out[h], 16 * U * QUADS)

        @block.gpsimd
        def _(pool):
            step = Steps(pool, "pool", pool_step)
            step(pool.memset(ident[:, :], 0.0))
            step(pool.memset(down[:, :], 0.0))
            step(pool.memset(up[:, :], 0.0))
            step(pool.memset(heads[:, :], 0.0))
            step(pool.memset(turn[:, :, :], 1.0))
            step(pool.memset(signs[:, :], 1.0))
            step(pool.memset(epsc[:, :], EPS))
            step(pool.iota(sign_i[:, 0:1], [[0, 1]], base=0, channel_multiplier=1))
            for index in (dst_i, src_i, out_i, row_i, back_i):
                step(pool.memset(index[:, TILES:TILES + U], 0))
            step(pool.iota(seqno, [[1, SORT]], base=0, channel_multiplier=SORT))
            step(pool.iota(place[:, :].bitcast(I32), [[1, 2], [TILES, P]], base=0, channel_multiplier=2))
            step(pool.iota(bound.bitcast(I32), [[REACH, GROUPS], [0, U]], base=REACH, channel_multiplier=0))
            step.settle()
            for m, base in ((ident, 0), (down, 1), (up, -1)):
                step(pool.affine_select(out=m[:, :], in_=m[:, :], compare_op=ALU.not_equal, fill=1.0, base=base,
                                        pattern=[[-1, P]], channel_multiplier=1))
            step.settle()
            for h in range(H):
                step(pool.memset(heads[DH * h:DH * h + DH, h:h + 1], 1.0 / math.sqrt(DH)))
                step.settle()
            for k in range(4):
                w = 2 ** k
                v = turn[:, k, :].rearrange("p (n q) -> p n q", q=4 * w)
                step(pool.memset(v[:, :, w:3 * w], -1.0))
            step(pool.memset(turn[:, 4, :].rearrange("p (n q) -> p n q", q=32)[:, :, 16:32], -1.0))
            step.settle()
            for q in range(4):
                b13, b14 = q & 1, q >> 1
                for col, s in ((1, b13), (2, b14), (3, b13 ^ b14)):
                    if s:
                        step(pool.memset(signs[32 * q:32 * q + 32, col:col + 1], -1.0))
                        step.settle()
            pool.sem_inc(consts, 1)

            def stream(index, free, issue):
                step(pool.tensor_copy(stage[:, 0, :], index[:, 0:U]))

                def groups(i):
                    for h in range(4):
                        g = 4 * i + h
                        free(g, h, i)
                        step(pool.tensor_copy(stage[:, (h + 1) % 4, :], index[:, bass.ds((g + 1) * U, U)]))
                        step.until(step.local - 1)
                        issue(g, h, i, lambda k: bass.IndirectOffsetOnAxis(ap=stage[:, h, k:k + 1], axis=0))
                step.loop(pool, 0, QUADS, groups)

            def gather(table, index, out, width, done, free):
                def issue(g, h, i, at):
                    r = h % 2
                    for k in range(U):
                        pool.indirect_dma_start(out=out[:, r, k * width:(k + 1) * width], out_offset=None, in_=table,
                                                in_offset=at(k)).then_inc(done[r], 16)
                stream(index, free, issue)

            pool.wait_ge(indexed, 1)
            gather(x[:, :], dst_i, rows, D, kd_in, lambda g, h, i: hold(pool, "pool", kd_turned, g - 1))

            pool.wait_ge(kd_turned, GROUPS)
            gather(x[:, :], src_i, rows, D, qs_in, lambda g, h, i: hold(pool, "pool", qs_turned, g - 1))

            pool.wait_ge(qs_turned, GROUPS)
            pool.wait_ge(late_ready, 1)
            late = pool.value_load(late_i[0:1, 0:1], min_val=0, max_val=ROWS)
            pool.wait_ge(indexed, 2)
            pool.wait_ge(scores_out, 16)
            gather(scores_d[:, :], row_i, small, H, g_in, lambda g, h, i: hold(pool, "pool", g_kept, g - 1))

            pool.wait_ge(g_kept, GROUPS)
            pool.wait_ge(back_in, 16)
            pool.wait_ge(alpha_out, 16)
            gather(alpha_d[:, :], back_i, small, H, a_in, lambda g, h, i: hold(pool, "pool", o_made, g - 1))

            def reused(g, h, i):
                hold(pool, "pool", e_out[(h + 1) % 4], (i + (h == 3)) * 16 * U)

            def scatter(g, h, at):
                hold(pool, "pool", e_done, g + 1)
                for k in range(U):
                    pool.indirect_dma_start(out=y[:, :], out_offset=at(k), in_=final_rows[h][:, k * D:(k + 1) * D],
                                            in_offset=None, bounds_check=N - 1, oob_is_err=False).then_inc(e_out[h], 16)

            def scatter_stored(g, h, i, at):
                hold(pool, "pool", d_out[h], (i + 1) * 16)
                scatter(g, h, at)

            before = step.n, step.local
            with pool.If(late > 0):
                for h in range(4):
                    pool.wait_ge(d_out[h], 16 * QUADS)
                stream(out_i, reused, lambda g, h, i, at: scatter(g, h, at))
            step.n, step.local = before
            with pool.Else():
                stream(out_i, reused, scatter_stored)

        @block.scalar
        def _(act):
            step = Steps(act, "act", act_step)
            act.wait_ge(biases_in, 16 * 8)

            def keys(i):
                for h in range(2):
                    g = 2 * i + h
                    hold(act, "act", kd_turned, g + 1)
                    hold(act, "act", k_made, g - 1)
                    act.activation(ringA[:, h, :], PS[0][:, 0:GW], ACT.Identity).then_inc(kx_ready, 1)
                    hold(act, "act", kd_saved[h], i * 16)
                    hold(act, "act", kx_ready, g + 1)
                    act.activation(ringB[:, h, :], ringA[:, h, :], ACT.Identity, bias=b2c[:, 0:1]).then_inc(kb_kept, 1)
                    hold(act, "act", k_made, g + 1)
                    act.activation(group(big, g), PS[1][:, 0:GW], ACT.Identity, bias=bkc[:, 0:1]).then_inc(k_kept, 1)
            keys(0)
            with act.Fori(1, PAIRS) as i:
                keys(i)
            act.wait_ge(k_made, GROUPS)

            def scores(i):
                for h in range(2):
                    g = 2 * i + h
                    hold(act, "act", qs_turned, g + 1)
                    hold(act, "act", m_made, g - 1)
                    act.activation(ringA[:, h, :], PS[0][:, 0:GW], ACT.Identity).then_inc(qx_ready, 1)
            scores(0)
            with act.Fori(1, PAIRS) as i:
                scores(i)

            act.wait_ge(late_ready, 1)
            late = act.value_load(late_i[0:1, 0:1], min_val=0, max_val=ROWS)
            act.wait_ge(soft_act, 1)
            act.activation(seg[0:SR, 0:H * SORT], bwd[0:SR, 0:H * SORT], ACT.Exp).then_inc(soft_exp, 1)

            def square(i):
                for h in range(2):
                    g = 2 * i + h
                    hold(act, "act", h_kept, g + 1)
                    step.settle()
                    step(act.activation(rows[:, h, :], group(big, g), ACT.Square,
                                        accum_out=sums[:, 1, bass.ds(g, 1)]))
                    act.sem_inc(pace["act"], 1)
            step.loop(act, 0, PAIRS, square)
            step.settle()
            act.sem_inc(squares, 1)

            act.wait_ge(bn_var, 1)
            act.activation(bn[:, 3:4], bn[:, 2:3], ACT.Sqrt, bias=epsc[:, 0:1]).then_inc(bn_sd, 1)
            act.wait_ge(bn_bias, 1)
            act.activation(bn[:, 8:9], bn[:, 7:8], ACT.Relu).then_inc(bn_rest, 1)

            def normalise(n, k, data, out, done):
                for j in range(n):
                    ins = act.activation(out[:, j * D:(j + 1) * D], data[:, j * D:(j + 1) * D], ACT.Identity,
                                         bias=lnsm[:, k, 6, j:j + 1], scale=lnsm[:, k, 5, j:j + 1])
                ins.then_inc(done, 1)

            def root(n, k, var, count, sd):
                hold(act, "act", var, count)
                act.activation(lnsm[:, k, 4, 0:n], lnsm[:, k, 3, 0:n], ACT.Sqrt, scale=1.0 / D,
                               bias=epsc[:, 0:1]).then_inc(sd, 1)

            def chunk_rows(c, h):
                hold(act, "act", d_scale, c + 1)
                normalise(CA, h, xin[h], xin[h], d_done)

            def relu(g, h):
                hold(act, "act", e_made, g - 1)
                act.activation(ringA[:, h % 2, :], group(big, g), ACT.Relu, bias=bn[:, 7:8],
                               scale=bn[:, 5:6]).then_inc(e_relu, 1)

            def final(g, h, scattered):
                hold(act, "act", e_scale, g + 1)
                hold(act, "act", e_out[h], scattered * 16 * U)
                normalise(U, 4 + h, PS[h], final_rows[h], e_done)

            def after(s, h, i, dense, edge, two_ago, three_ago):
                p2, p3 = (h - 2) % 4, (h - 3) % 4
                if edge and two_ago:
                    root(U, 4 + p2, e_var, s - 1, e_sd)
                if dense and three_ago:
                    chunk_rows(s - 3, p3)
                if edge and two_ago:
                    final(s - 2, p2, i - (h < 2))
                if dense and two_ago:
                    root(CN, p2, d_var, s - 1, d_sd)

            def turns(i, dense, edge):
                for h in range(4):
                    s = 4 * i + h
                    if edge:
                        relu(s, h)
                    old = s if isinstance(s, int) else CHUNKS
                    after(s, h, i, dense, edge, old >= 2, old >= 3)

            def work(dense, edge):
                turns(0, dense, edge)
                with act.Fori(1, QUADS) as i:
                    turns(i, dense, edge)
                for s in range(GROUPS, GROUPS + 3):
                    after(s, s % 4, s // 4, dense, edge, s < GROUPS + 2, True)

            act.wait_ge(h_made, GROUPS)
            with act.If(late > 0):
                work(True, False)
                work(False, True)
            with act.Else():
                work(True, True)

        @block.vector
        def _(dve):
            step = Steps(dve, "dve", dve_step)

            def two(view, w):
                return view.rearrange("p (n two s) -> p n two s", two=2, s=w)

            def exchange(a, b, w):
                ia, ib = two(a, w), two(b, w)
                step.settle()
                step(dve.tensor_tensor(ib[:, :, 0, :], ia[:, :, 0, :], ia[:, :, 1, :], ALU.min))
                step(dve.tensor_tensor(ib[:, :, 1, :], ia[:, :, 0, :], ia[:, :, 1, :], ALU.max))
                return b, a

            def mirror(a, b, w):
                ia, ib = two(a, w), two(b, w)
                step.settle()
                step(dve.tensor_tensor(ib[:, :, 0, :], ia[:, :, 0, :], ia[:, :, 1, ::-1], ALU.min))
                step(dve.tensor_tensor(ib[:, :, 1, :], ia[:, :, 0, ::-1], ia[:, :, 1, :], ALU.max))
                return b, a

            def sign(a, b, col):
                step.settle()
                step(dve.tensor_scalar(b, a, signs[:, col:col + 1], None, ALU.mult))
                return b, a

            def sort(a, b):
                a, b = sign(a, b, 0)
                for k in range(1, 9):
                    a, b = mirror(a, b, 2 ** (k - 1))
                    for j in range(k - 2, -1, -1):
                        a, b = exchange(a, b, 2 ** j)
                for k in range(9, 16):
                    step.settle()
                    step(dve.transpose(b, a))
                    a, b = b, a
                    if k < 14:
                        step.settle()
                        step(dve.tensor_tensor(b, a, turn[:, k - 9, :], ALU.mult))
                        a, b = b, a
                    if k == 13:
                        a, b = sign(a, b, 1)
                    if k == 14:
                        a, b = sign(a, b, 3)
                    if k == 15:
                        a, b = sign(a, b, 2)
                    for j in range(k - 1, 12, -1):
                        step.settle()
                        for q in range(4):
                            o = q ^ (1 << (j - 13))
                            s = -1.0 if (q >> (j - 13)) & 1 else 1.0
                            step(dve.tensor_scalar(b[32 * q:32 * q + 32, :], a[32 * o:32 * o + 32, :], s, None,
                                                   ALU.mult))
                        step.settle()
                        step(dve.scalar_tensor_tensor(t1, a, signs[:, j - 12:j - 11], b, ALU.mult, ALU.min))
                        step.settle()
                        step(dve.tensor_scalar(b, t1, signs[:, j - 12:j - 11], None, ALU.mult))
                        a, b = b, a
                    for j in range(min(k - 1, 12), 7, -1):
                        a, b = exchange(a, b, 2 ** (j - 8))
                    step.settle()
                    step(dve.transpose(b, a))
                    a, b = b, a
                    for j in range(7, -1, -1):
                        a, b = exchange(a, b, 2 ** j)
                step.settle()
                return a

            def high(values, tmp1, tmp2, out):
                step.settle()
                step(dve.tensor_scalar(tmp1, values, float(HALF), None, ALU.is_ge))
                step(dve.tensor_scalar(tmp2, values, 2.0, -float(2 * HALF + 32767), ALU.mult, ALU.add))
                step.settle()
                step(dve.tensor_tensor(tmp1, tmp1, tmp2, ALU.mult))
                step.settle()
                step(dve.tensor_scalar(tmp2, values, -1.0, float(HALF + 32895), ALU.mult, ALU.add))
                step.settle()
                step(dve.tensor_tensor(out, tmp1, tmp2, ALU.add))

            def unpack(v):
                lo, hi = v.bitcast(U16)[:, 0::2], v.bitcast(U16)[:, 1::2]
                step(dve.tensor_copy(pay, lo))
                step(dve.tensor_scalar(t1, hi, 32768.0, None, ALU.is_ge))
                step(dve.tensor_scalar(t2, hi, -2.0, float(2 * HALF + 32895 - HALF + 128 - HALF), ALU.mult, ALU.add))
                step(dve.tensor_scalar(key, hi, float(HALF - 128), None, ALU.add))
                step.settle()
                step(dve.tensor_tensor(t1, t1, t2, ALU.mult))
                step.settle()
                step(dve.tensor_tensor(key, key, t1, ALU.add))
                step.settle()
                step(dve.tensor_scalar(key1, key, 1.0, None, ALU.add))
                step.settle()

            def mark(same, n):
                dve.sem_inc(sorted_keys, 1)
                step(dve.tensor_tensor(same[:, 1:SORT], key1[:, 1:SORT], key1[:, 0:SORT - 1], ALU.is_equal))
                dve.wait_ge(shifted, 2 * n + 1)
                step(dve.tensor_tensor(same[:, 0:1], key1[:, 0:1], PS[0][:, 0:1], ALU.is_equal))
                step.settle()
                dve.sem_inc(marks, 1)
                dve.wait_ge(shifted, 2 * n + 2)
                rows_ = P if n == 0 else SR
                step(dve.tensor_copy(same[0:rows_, SORT:SORT + 1], PS[0][0:rows_, 2:3]))
                step.settle()

            step(dve.memset(raw, N))
            step.settle()
            dve.sem_inc(raw_clear, 1)
            dve.wait_ge(consts, 1)
            step(dve.tensor_scalar(sign_i[:, 1:2], sign_i[:, 0:1], 1, None, ALU.bitwise_and))
            step.settle()
            step(dve.tensor_scalar(signs[:, 0:1], sign_i[:, 1:2], -2.0, 1.0, ALU.mult, ALU.add))
            dve.wait_ge(lists_in, 64)
            step(dve.tensor_copy(key, raw[:, 0:SORT]))
            step(dve.tensor_scalar(key1, raw[:, 0:SORT], 1.0, None, ALU.add))
            step(dve.tensor_copy(pay, raw[:, SORT:2 * SORT]))
            step.settle()
            dve.sem_inc(order_pe, 1)
            step(dve.tensor_tensor(t1[:, 1:SORT], key1[:, 1:SORT], key1[:, 0:SORT - 1], ALU.is_lt))
            dve.wait_ge(order_dve, 1)
            step(dve.tensor_tensor(t1[:, 0:1], key1[:, 0:1], PS[0][:, 0:1], ALU.is_lt))
            step.settle()
            step(dve.tensor_reduce(pack[:, 0:1], t1, AX.X, ALU.add))
            step.settle()
            dve.sem_inc(order_pe, 1)
            dve.wait_ge(order_dve, 2)
            step(dve.tensor_copy(one_i[0:1, 0:1], PS[0][0:1, 4:5]))
            step.settle()
            falls = dve.value_load(one_i[0:1, 0:1], min_val=0, max_val=E)
            before = step.local
            with dve.If(falls > 0):
                lo, hi = va.bitcast(U16)[:, 0::2], va.bitcast(U16)[:, 1::2]
                high(key, t1, t2, hi)
                step(dve.tensor_copy(lo, pay))
                v = sort(va, vb)
                unpack(v)
            with dve.Else():
                dve.sem_inc(dve_step, step.local - before)
            mark(same1, 0)
            step(dve.tensor_copy(same16, same1[:, 0:SORT]))
            step(dve.scalar_tensor_tensor(t2, same1[:, 1:SORT + 1], float(SKIP), key, ALU.mult, ALU.add))
            step.settle()
            dve.sem_inc(marks, 1)
            dve.wait_ge(turned, 1)
            for m, (dest, top) in enumerate(((dst_i, N - 1.0), (src_i, N - 1.0), (out_i, 2.0 * SKIP))):
                psv = PS[m][:, 0:2 * P].rearrange("p (c t) -> p c t", c=2)[:, :, 0:SR]
                step(dve.tensor_scalar(dest[:, 0:TILES].rearrange("p (t c) -> p c t", c=2), psv, top, None, ALU.min))
            step.settle()
            dve.sem_inc(indexed, 1)

            step(dve.tensor_copy(bound, bound.bitcast(I32)))
            step(dve.tensor_copy(ends, dst_i[:, 0:TILES]))
            step.settle()
            step(dve.tensor_tensor(ends, ends, bound, ALU.is_ge))
            step.settle()
            step(dve.tensor_reduce(counted, ends[:, 0:TILES - U], AX.X, ALU.add))
            step.settle()
            dve.sem_inc(late_pe, 1)

            step(dve.tensor_copy(t1, place[:, :].bitcast(I32)))
            step.settle()
            step(dve.tensor_copy(key, pay))
            step(dve.tensor_scalar(t2[:, 0:1], sign_i[:, 0:1], float(SR), None, ALU.is_ge))
            step.settle()
            step(dve.tensor_scalar(t2[:, 0:1], t2[:, 0:1], float(ROWS), None, ALU.mult))
            step.settle()
            v0 = va if v is vb else vb
            other = v
            lo, hi = v0.bitcast(U16)[:, 0::2], v0.bitcast(U16)[:, 1::2]
            step(dve.tensor_scalar(lo, t1, t2[:, 0:1], None, ALU.add))
            step.settle()
            high(key, t1, t2, hi)
            v = sort(v0, other)
            unpack(v)
            step(dve.tensor_copy(later, pay))
            free = va if v is vb else vb
            lo, hi = free.bitcast(U16)[:, 0::2], free.bitcast(U16)[:, 1::2]
            step(dve.tensor_copy(lo, seqno))
            high(later, t1, t2, hi)
            w = sort(free, v)
            step(dve.tensor_copy(way, w.bitcast(U16)[:, 0::2]))
            step.settle()
            dve.sem_inc(way_ready, 1)

            mark(same2, 1)
            dve.sem_inc(marks, 1)
            dve.wait_ge(late_dve, 1)
            step(dve.tensor_copy(late_i[0:1, 0:1], PS[3][0:1, 0:1]))
            step.settle()
            dve.sem_inc(late_ready, 1)
            late = dve.value_load(late_i[0:1, 0:1], min_val=0, max_val=ROWS)
            dve.wait_ge(turned, 2)
            psv = PS[0][:, 0:2 * P].rearrange("p (c t) -> p c t", c=2)[:, :, 0:SR]
            step(dve.tensor_scalar(row_i[:, 0:TILES].rearrange("p (t c) -> p c t", c=2), psv, ROWS - 1.0, None, ALU.min))
            step.settle()
            dve.sem_inc(indexed, 1)

            def scores(i):
                for h in range(2):
                    g = 2 * i + h
                    hold(dve, "dve", q_made, g + 1)
                    hold(dve, "dve", s_made, g - 1)
                    dve.scalar_tensor_tensor(ringB[:, h, :], PS[1][:, 0:GW], bqc[:, 0:1], group(big, g),
                                             ALU.add, ALU.mult).then_inc(qk_ready, 1)
                    hold(dve, "dve", m_made, g + 1)
                    hold(dve, "dve", qk_ready, g + 1)
                    dve.tensor_tensor(group(big, g).rearrange("p (n d) -> p n d", d=D),
                                      PS[2][:, 0:GW].rearrange("p (n d) -> p n d", d=D),
                                      bmr[:, :].unsqueeze(1).to_broadcast([P, U, D]), ALU.add).then_inc(m_kept, 1)
                    hold(dve, "dve", s_made, g + 1)
                    dve.tensor_copy(sc[:, bass.ds(g * U * H, U * H)], PS[3][:, 0:U * H]).then_inc(s_kept, 1)
            dve.wait_ge(k_kept, GROUPS)
            for h in range(2):
                dve.wait_ge(kd_saved[h], 16 * PAIRS)
            dve.wait_ge(biases_in, 16 * 8)
            scores(0)
            with dve.Fori(1, PAIRS) as i:
                scores(i)

            sp_, sn_ = same2[0:SR, 0:SORT], same2[0:SR, 1:SORT + 1]
            K = H + 1
            segv = seg[0:SR, :].rearrange("p (j f) -> p j f", j=K)
            fwdv = fwd[0:SR, :].rearrange("p (j f) -> p j f", j=K)
            bwdv = bwd[0:SR, :].rearrange("p (j f) -> p j f", j=K)
            ng = negs[0:SR, :]
            whole_before, whole_low, whole_after = (pack[0:SR, j:j + 1] for j in (9, 10, 11))
            turn_no = [0]

            def cross(a, b, back, last, whole, start, op0, op1):
                n = b - a
                step.settle()
                step(dve.tensor_copy(pack[0:SR, 0:n].unsqueeze(2), last))
                step(dve.tensor_copy(pack[0:SR, H:H + n], whole.to_broadcast([SR, n])))
                step(dve.memset(cscan[0:n, SR:SR + 1] if back else cscan[0:n, 0:1], start))
                step.settle()
                dve.sem_inc(soft_pe, 1)
                turn_no[0] += 1
                dve.wait_ge(soft_dve, turn_no[0])
                step(dve.tensor_copy(crow[0:n, :].rearrange("p (a n) -> p a n", a=2)[:, :, 0:SR],
                                     PS[3][0:n, 0:2 * P].rearrange("p (a n) -> p a n", a=2)[:, :, 0:SR]))
                step.settle()
                m, v = crow[0:n, P:P + SR], crow[0:n, 0:SR]
                if back:
                    step(dve.tensor_tensor_scan(cscan[0:n, 0:SR][:, ::-1], m[:, ::-1], v[:, ::-1], start, op0, op1))
                else:
                    step(dve.tensor_tensor_scan(cscan[0:n, 1:SR + 1], m, v, start, op0, op1))
                step.settle()
                dve.sem_inc(soft_pe, 1)
                turn_no[0] += 1
                dve.wait_ge(soft_dve, turn_no[0])
                step(dve.tensor_copy(carry[0:SR, 0:n], PS[3][0:SR, 512:512 + n]))
                step.settle()

            def forward(a, b, mask, start, op0, op1, whole):
                step.settle()
                for j in range(a, b):
                    step(dve.tensor_tensor_scan(fwdv[:, j, :], mask, segv[:, j, :], start, op0, op1))
                cross(a, b, False, fwdv[:, a:b, SORT - 1:SORT], whole, start, op0, op1)
                for j in range(a, b):
                    step(dve.tensor_tensor_scan(fwdv[:, j, :], mask, segv[:, j, :], carry[0:SR, j - a:j - a + 1],
                                                op0, op1))
                step.settle()

            def backward(a, b):
                for j in range(a, b):
                    step(dve.scalar_tensor_tensor(fwdv[:, j, :], sn_, 0.0, fwdv[:, j, :], ALU.is_equal, ALU.mult))
                step.settle()
                for j in range(a, b):
                    step(dve.tensor_tensor_scan(bwdv[:, j, ::-1], sn_[:, ::-1], fwdv[:, j, ::-1], 0.0,
                                                ALU.mult, ALU.add))
                cross(a, b, True, bwdv[:, a:b, 0:1], whole_after, 0.0, ALU.mult, ALU.add)
                for j in range(a, b):
                    step(dve.tensor_tensor_scan(bwdv[:, j, ::-1], sn_[:, ::-1], fwdv[:, j, ::-1],
                                                carry[0:SR, j - a:j - a + 1], ALU.mult, ALU.add))
                step.settle()

            step(dve.tensor_scalar(ng, sp_, 1.0, -LOW, ALU.subtract, ALU.mult))
            step(dve.memset(segv[:, H, :], 1.0))
            step(dve.tensor_reduce(whole_before, sp_, AX.X, ALU.min))
            step(dve.tensor_reduce(whole_after, sn_, AX.X, ALU.min))
            step.settle()
            step(dve.tensor_scalar(whole_low, whole_before, 1.0, -LOW, ALU.subtract, ALU.mult))
            forward(H, K, sp_, 0.0, ALU.mult, ALU.add, whole_before)
            backward(H, K)

            def take_scores(i):
                for h in range(2):
                    g = 2 * i + h
                    hold(dve, "dve", g_in[h], (i + 1) * 16 * U)
                    dve.tensor_copy(gs[:, :, bass.ds(g * U, U)],
                                    small[:, h, :].rearrange("p (t h) -> p h t", h=H)).then_inc(g_kept, 1)
            take_scores(0)
            with dve.Fori(1, PAIRS) as i:
                take_scores(i)
            turn_no[0] += 1
            dve.wait_ge(soft_dve, turn_no[0])
            step(dve.tensor_copy(seg[0:SR, 0:H * SORT], PS[0][0:SR, 0:H * SORT]))
            forward(0, H, ng, LOW, ALU.add, ALU.max, whole_low)
            backward(0, H)
            step(dve.tensor_tensor(bwd[0:SR, 0:H * SORT], seg[0:SR, 0:H * SORT], bwd[0:SR, 0:H * SORT], ALU.subtract))
            step.settle()
            dve.sem_inc(soft_act, 1)
            dve.wait_ge(soft_exp, 1)
            forward(0, H, sp_, 0.0, ALU.mult, ALU.add, whole_before)
            backward(0, H)
            for j in range(H):
                step(dve.reciprocal(fwdv[:, j, :], bwdv[:, j, :]))
                step(dve.tensor_tensor(segv[:, j, :], segv[:, j, :], bwdv[:, H, :], ALU.mult))
            step.settle()
            for j in range(H):
                step(dve.tensor_tensor(bwd[0:SR, j:H * SORT:H], segv[:, j, :], fwdv[:, j, :], ALU.mult))
            step.settle()
            dve.sem_inc(weights_ready, 1)

            def weigh(g, h, i):
                hold(dve, "dve", a_in[h], i * 16 * U)
                hold(dve, "dve", o_turned, g - 1)
                dve.tensor_tensor(ringA[:, h, :].rearrange("p (n d) -> p n d", d=DH),
                                  group(big, g).rearrange("p (n d) -> p n d", d=DH),
                                  small[:, h, :].unsqueeze(2).to_broadcast([P, U * H, DH]),
                                  ALU.mult).then_inc(o_made, 1)

            def scan(g, h, i):
                hold(dve, "dve", o_turned, g + 1)
                hold(dve, "dve", f_in[h], i * 16)
                hold(dve, "dve", h_made, g - 1)
                hold(dve, "dve", run_sums, g)
                first = isinstance(g, int) and g == 0
                r = h % 2
                dve.tensor_tensor_scan(ringB[:, r, :], flags[:, h, 0:GW], PS[2 * r][:, 0:GW],
                                       0.0 if first else ringB[:, 1 - r, GW - 1:GW],
                                       ALU.mult, ALU.add).then_inc(run_sums, 1)

            def keep(g, h):
                hold(dve, "dve", h_made, g + 1)
                dve.scalar_tensor_tensor(group(big, g), flags[:, h, 1:GW + 1], 0.0, PS[2 * (h % 2) + 1][:, 0:GW],
                                         ALU.is_equal, ALU.mult,
                                         accum_out=sums[:, 0, bass.ds(g, 1)]).then_inc(h_kept, 1)

            def run_group(i):
                for h in range(4):
                    g = 4 * i + h
                    weigh(g, h % 2, 2 * i + h // 2 + 1)
                    if not isinstance(g, int) or g > 0:
                        scan(g - 1, (h - 1) % 4, i + (h > 0))
                    if not isinstance(g, int) or g > 1:
                        keep(g - 2, (h - 2) % 4)
            run_group(0)
            with dve.Fori(1, QUADS) as i:
                run_group(i)
            scan(GROUPS - 1, 3, QUADS)
            keep(GROUPS - 2, 2)
            keep(GROUPS - 1, 3)

            dve.wait_ge(squares, 1)
            dve.wait_ge(h_kept, GROUPS)
            step(dve.tensor_reduce(bn[:, 0:2], sums[:, :, :], AX.X, ALU.add))
            step.settle()
            step(dve.tensor_scalar(bn[:, 0:2], bn[:, 0:2], 1.0 / N, None, ALU.mult))
            step.settle()
            step(dve.tensor_tensor(bn[:, 4:5], bn[:, 0:1], bn[:, 0:1], ALU.mult))
            step(dve.tensor_tensor(bn[:, 6:7], bn[:, 0:1], b1c[:, 0:1], ALU.add))
            step.settle()
            step(dve.tensor_tensor(bn[:, 2:3], bn[:, 1:2], bn[:, 4:5], ALU.subtract))
            step.settle()
            dve.sem_inc(bn_var, 1)
            dve.wait_ge(bn_sd, 1)
            step(dve.reciprocal(bn[:, 4:5], bn[:, 3:4]))
            step(dve.tensor_tensor(bn[:, 6:7], b1c[:, 0:1], bn[:, 6:7], ALU.subtract))
            step.settle()
            step(dve.tensor_tensor(bn[:, 5:6], bn[:, 4:5], gammac[:, 0:1], ALU.mult))
            step.settle()
            step(dve.scalar_tensor_tensor(bn[:, 7:8], bn[:, 6:7], bn[:, 5:6], betac[:, 0:1], ALU.mult, ALU.add))
            step.settle()
            dve.sem_inc(bn_bias, 1)
            dve.wait_ge(rest_made, 1)
            step(dve.tensor_tensor(rest[:, :], PS[2][:, 0:D], b2r[:, :], ALU.add))
            step.settle()
            dve.sem_inc(rest_ready, 1)

            def bn_rows(n, k, data, a, b):
                for j in range(a, b):
                    step(dve.bn_stats(lnst[:, k, 6 * j:6 * j + 6], data[:, j * D:(j + 1) * D]))

            def halves(n, k):
                st = lnst[:, k, 0:6 * n].rearrange("p (n s) -> p n s", s=6)
                q = lnsm[:, k, :, 0:n]
                step(dve.tensor_tensor(q[:, 0, :], st[:, :, 1], st[:, :, 4], ALU.add))
                step(dve.tensor_tensor(q[:, 1, :], st[:, :, 1], st[:, :, 4], ALU.subtract))
                step(dve.tensor_tensor(q[:, 2, :], st[:, :, 2], st[:, :, 5], ALU.add))

            def square(n, k):
                q = lnsm[:, k, :, 0:n]
                step(dve.tensor_tensor(q[:, 1, :], q[:, 1, :], q[:, 1, :], ALU.mult))

            def variance(n, k, var):
                q = lnsm[:, k, :, 0:n]
                dve.scalar_tensor_tensor(q[:, 3, :], q[:, 1, :], D / 4.0, q[:, 2, :],
                                         ALU.mult, ALU.add).then_inc(var, 1)

            def inverse(n, k, sd, count, done, used):
                hold(dve, "dve", done, used)
                hold(dve, "dve", sd, count)
                q = lnsm[:, k, :, 0:n]
                step(dve.reciprocal(q[:, 5, :], q[:, 4, :]))

            def offset(n, k, scale):
                q = lnsm[:, k, :, 0:n]
                dve.scalar_tensor_tensor(q[:, 6, :], q[:, 0, :], -0.5, q[:, 5, :],
                                         ALU.mult, ALU.mult).then_inc(scale, 1)

            def share(c, k):
                hold(dve, "dve", d_scale, c + 1)
                for j in range(CA, CN):
                    row = xin[k][:, j * D:(j + 1) * D]
                    ins = dve.tensor_scalar(row, row, lnsm[:, k, 5, j:j + 1], lnsm[:, k, 6, j:j + 1],
                                            ALU.mult, ALU.add)
                    if j < CN - 1:
                        step(ins)
                ins.then_inc(d_part, 1)

            def turn_of(s, h, i, dense, edge):
                some = not isinstance(s, int) or s > 0
                p = (h - 1) % 4
                base = step.local

                def small(there, n, body, after=None):
                    if there and some:
                        if after is not None:
                            step.until(after)
                        body()
                        assert step.local == mark_[0] + n
                    elif there:
                        step.skip(n)
                    mark_[0] = step.local

                mark_ = [0]

                def at():
                    mark_[0] = step.local
                    return step.local

                if dense:
                    hold(dve, "dve", d_in[h], (i + 1) * 16)
                    v = xin[h].rearrange("p (n d) -> p n d", d=D)
                    step(dve.tensor_tensor(v, v, rest[:, :].unsqueeze(1).to_broadcast([P, CN, D]), ALU.add))
                added = at()
                small(dense, 3, lambda: halves(CN, p), base)
                halved = at()
                small(edge, 1, lambda: inverse(U, 4 + p, e_sd, s, e_done, s - 4))
                inverted = at()
                if edge:
                    hold(dve, "dve", e_made, s + 1)
                    bn_rows(U, 4 + h, PS[h], 0, 3)
                at()
                small(dense, 1, lambda: square(CN, p), halved)
                squared = at()
                if edge and some:
                    step.until(inverted)
                    offset(U, 4 + p, e_scale)
                if edge:
                    bn_rows(U, 4 + h, PS[h], 3, 5)
                if dense and some:
                    step.until(squared)
                    variance(CN, p, d_var)
                if edge:
                    bn_rows(U, 4 + h, PS[h], 5, U)
                known = step.local
                if dense:
                    step.until(added)
                    bn_rows(CN, h, xin[h], 0, 4)
                if edge:
                    step.until(known)
                    halves(U, 4 + h)
                halved = step.local
                if dense:
                    bn_rows(CN, h, xin[h], 4, 7)
                if edge:
                    step.until(halved)
                    square(U, 4 + h)
                squared = step.local
                if dense:
                    bn_rows(CN, h, xin[h], 7, 9)
                if edge:
                    step.until(squared)
                    variance(U, 4 + h, e_var)
                if dense:
                    bn_rows(CN, h, xin[h], 9, 12)
                at()
                small(dense, 1, lambda: inverse(CN, p, d_sd, s, d_done, s - 4))
                inverted = at()
                if dense:
                    bn_rows(CN, h, xin[h], 12, CN)
                    if some:
                        step.until(inverted)
                        offset(CN, p, d_scale)
                at()
                small(dense, CN - CA - 1, lambda: share(s - 1, p))

            def work(dense, edge):
                def turns(i):
                    for h in range(4):
                        turn_of(4 * i + h, h, i, dense, edge)
                step.loop(dve, 0, QUADS, turns)
                step.settle()
                last = 3
                if edge:
                    inverse(U, 4 + last, e_sd, GROUPS, e_done, GROUPS - 4)
                if dense:
                    halves(CN, last)
                    step.settle()
                    square(CN, last)
                    step.settle()
                    variance(CN, last, d_var)
                if edge:
                    step.settle()
                    offset(U, 4 + last, e_scale)
                if dense:
                    inverse(CN, last, d_sd, CHUNKS, d_done, CHUNKS - 4)
                    step.settle()
                    offset(CN, last, d_scale)
                    share(CHUNKS - 1, last)
                step.settle()

            before = step.n, step.local
            with dve.If(late > 0):
                work(True, False)
                work(False, True)
            step.n, step.local = before
            with dve.Else():
                work(True, True)

        @block.tensor
        def _(pe):
            pe.wait_ge(consts, 1)

            def wide(out, w, data):
                pe.matmul(out[:, 0:512], w[:, :], data[:, 0:512], start=True, stop=True)
                return pe.matmul(out[:, 512:GW], w[:, :], data[:, 512:GW], start=True, stop=True)

            def flip(out, data):
                for k in range(U):
                    last = pe.transpose(out[:, k * P:(k + 1) * P], data[:, k * P:(k + 1) * P], ident[:, :])
                return last

            def after_sort(n):
                pe.wait_ge(sorted_keys, n + 1)
                if n:
                    pe.wait_ge(kx_ready, GROUPS)
                    pe.wait_ge(k_kept, GROUPS)
                pe.matmul(PS[0][:, 0:1], down[:, :], key1[:, SORT - 1:SORT], start=True, stop=True).then_inc(shifted, 1)
                pe.wait_ge(marks, 2 * n + 1)
                same, r = (same1, P) if n == 0 else (same2, SR)
                pe.matmul(PS[0][0:r, 2:3], up[0:r, 0:r], same[0:r, 0:1], start=True, stop=True).then_inc(shifted, 1)
                pe.wait_ge(marks, 2 * n + 2)
                for m, t in enumerate((key, pay, t2) if n == 0 else (later,)):
                    for c in range(2):
                        last = pe.transpose(PS[m][:, c * P:(c + 1) * P], t[:, c * P:(c + 1) * P], ident[:, :])
                last.then_inc(turned, 1)

            pe.wait_ge(order_pe, 1)
            pe.matmul(PS[0][:, 0:1], down[:, :], key1[:, SORT - 1:SORT], start=True, stop=True).then_inc(order_dve, 1)
            pe.wait_ge(order_pe, 2)
            pe.matmul(PS[0][0:1, 4:5], pack[:, 0:1], signs[:, 4:5], start=True, stop=True).then_inc(order_dve, 1)

            after_sort(0)
            pe.wait_ge(indexed, 1)
            pe.wait_ge(weights_in, 16 * 5)

            def keys(i):
                for h in range(2):
                    g = 2 * i + h
                    hold(pe, "pe", kd_in[h], (i + 1) * 16 * U)
                    hold(pe, "pe", kx_ready, g)
                    flip(PS[0], rows[:, h, :]).then_inc(kd_turned, 1)
                    hold(pe, "pe", kx_ready, g + 1)
                    hold(pe, "pe", k_kept, g)
                    wide(PS[1], wk, ringA[:, h, :]).then_inc(k_made, 1)
            keys(0)
            with pe.Fori(1, PAIRS) as i:
                keys(i)
            pe.wait_ge(late_pe, 1)
            pe.matmul(PS[3][0:1, 0:1], counted, signs[:, 4:5], start=True, stop=True).then_inc(late_dve, 1)
            after_sort(1)
            pe.wait_ge(indexed, 2)

            def scores(i):
                for h in range(2):
                    g = 2 * i + h
                    hold(pe, "pe", qs_in[h], (i + 1) * 16 * U)
                    hold(pe, "pe", qx_ready, g)
                    flip(PS[0], rows[:, h, :]).then_inc(qs_turned, 1)
                    hold(pe, "pe", qx_ready, g + 1)
                    hold(pe, "pe", qk_ready, g)
                    wide(PS[1], wq, ringA[:, h, :]).then_inc(q_made, 1)
                    hold(pe, "pe", m_kept, g)
                    for k in range(U):
                        last = pe.matmul(PS[2][:, k * D:(k + 1) * D], ringA[:, h, k * P:(k + 1) * P], wm[:, :],
                                         start=True, stop=True)
                    last.then_inc(m_made, 1)
                    hold(pe, "pe", qk_ready, g + 1)
                    hold(pe, "pe", s_kept, g)
                    for k in range(U):
                        last = pe.matmul(PS[3][:, k * H:(k + 1) * H], ringB[:, h, k * P:(k + 1) * P], heads[:, :],
                                         start=True, stop=True)
                    last.then_inc(s_made, 1)
            scores(0)
            with pe.Fori(1, PAIRS) as i:
                scores(i)

            asked = [0]

            def cross(n, back):
                asked[0] += 1
                pe.wait_ge(soft_pe, asked[0])
                pe.transpose(PS[3][0:n, 0:SR], pack[0:SR, 0:n], ident[0:SR, 0:SR])
                pe.transpose(PS[3][0:n, P:P + SR], pack[0:SR, H:H + n], ident[0:SR, 0:SR]).then_inc(soft_dve, 1)
                asked[0] += 1
                pe.wait_ge(soft_pe, asked[0])
                at = 1 if back else 0
                pe.transpose(PS[3][0:SR, 512:512 + n], cscan[0:n, at:at + SR],
                             ident[0:n, 0:n]).then_inc(soft_dve, 1)

            pe.wait_ge(s_kept, GROUPS)
            cross(1, False)
            cross(1, True)
            pe.wait_ge(g_kept, GROUPS)
            for h in range(H):
                for c in range(2):
                    last = pe.transpose(PS[0][0:SR, (2 * h + c) * P:(2 * h + c + 1) * P],
                                        gs[:, h, :].rearrange("p (t c) -> p c t", c=2)[:, c, :], ident[:, :])
            last.then_inc(soft_dve, 1)
            for back in (False, True, False, True):
                cross(H, back)

            def flip_sums(g, h):
                hold(pe, "pe", o_made, g + 1)
                hold(pe, "pe", run_sums, g - 1)
                flip(PS[2 * h], ringA[:, h, :]).then_inc(o_turned, 1)

            def first_layer(g, h):
                hold(pe, "pe", run_sums, g + 1)
                hold(pe, "pe", h_kept, g - 1)
                wide(PS[2 * h + 1], w1, ringB[:, h, :]).then_inc(h_made, 1)

            flip_sums(0, 0)
            flip_sums(1, 1)
            first_layer(0, 0)
            with pe.Fori(1, PAIRS) as i:
                for h in range(2):
                    g = 2 * i + h
                    flip_sums(g, h)
                    first_layer(g - 1, 1 - h)
            first_layer(GROUPS - 1, 1)

            pe.wait_ge(bn_rest, 1)
            pe.matmul(PS[2][:, 0:D], bn[:, 8:9].to_broadcast([P, P]), w2[:, :], start=True, stop=True)\
              .then_inc(rest_made, 1)

            def edges(i):
                for h in range(4):
                    g = 4 * i + h
                    hold(pe, "pe", e_relu, g + 1)
                    hold(pe, "pe", e_in[h], (i + 1) * 16)
                    hold(pe, "pe", e_done, g - 3)
                    for k in range(U):
                        out = PS[h][:, k * D:(k + 1) * D]
                        pe.matmul(out, ringA[:, h % 2, k * P:(k + 1) * P], w2[:, :], start=True, stop=False)
                        last = pe.matmul(out, zring[:, h, k * P:(k + 1) * P], ident[:, :], start=False, stop=True)
                    last.then_inc(e_made, 1)
            pe.wait_ge(rest_ready, 1)
            edges(0)
            with pe.Fori(1, QUADS) as i:
                edges(i)


_NAMES = ["x", "src", "dst", "L0_gnn_Wk", "L0_gnn_bk", "L0_gnn_Wm", "L0_gnn_bm", "L0_gnn_Wq", "L0_gnn_bq",
          "L0_gnn_W1", "L0_gnn_b1", "L0_gnn_gamma", "L0_gnn_beta", "L0_gnn_W2", "L0_gnn_b2"]


def kernel(**inputs):
    import numpy as np
    import concourse.bacc as bacc
    from concourse.bass_utils import run_bass_kernel_spmd as run

    nc = bacc.Bacc("TRN2", target_bir_lowering=False, num_devices=1)
    arrays, args = {}, []
    for name in _NAMES:
        a = np.ascontiguousarray(inputs[name])
        arrays[f"in_{name}"] = a
        args.append(nc.dram_tensor(f"in_{name}", a.shape, mybir.dt.from_np(a.dtype), kind="ExternalInput").ap())
    y = nc.dram_tensor("y", (N, D), F32, kind="ExternalOutput").ap()
    build(nc, *args, y)
    return run(nc, [arrays], core_ids=[0]).results[0]["y"]
```

```python
import math
from contextlib import ExitStack

import concourse.bass as bass
from concourse import mybir

F32 = mybir.dt.float32
BF16 = mybir.dt.bfloat16
I32 = mybir.dt.int32
U16 = mybir.dt.uint16
ALU = mybir.AluOpType
ACT = mybir.ActivationFunctionType
AX = mybir.AxisListType

N = 50000
E = 25000
D = 128
H = 4
DH = D // H
EPS = 1e-5
P = 128
TILES = -(-E // P)
U = 7
GROUPS = TILES // U
PAIRS = GROUPS // 2
QUADS = GROUPS // 4
GW = U * P
ROWS = TILES * P
SORT = 256
SR = TILES // 2
LP = E // SORT
CN = 14
LR = CN + U
CHUNK = P * CN
CHUNKS = -(-N // CHUNK)
OVER = CHUNKS * CHUNK - N
CW = CN * D
LAG = 3
CA = 11
FEW = 12
ROOM = 9984
LOW = -1.0e30
SKIP = 100000
HALF = N // 2

assert CHUNKS == GROUPS
assert LAG == 3


def build(nc, x, src, dst, Wk, bk, Wm, bm, Wq, bq, W1, b1, gamma, beta, W2, b2, y):
    ctx = ExitStack()
    with ctx:
        def sb(name, shape, dt=F32):
            return ctx.enter_context(nc.sbuf_tensor(name, shape, dt))

        def sem(name):
            return ctx.enter_context(nc.semaphore(name))

        xdst_d = nc.dram_tensor("xdst_d", [GROUPS, P, GW], F32).ap()
        scores_d = nc.dram_tensor("scores_d", [ROWS, H], F32).ap()
        alpha_d = nc.dram_tensor("alpha_d", [ROWS, H], F32).ap()
        same_d = nc.dram_tensor("same_d", [P * SORT], BF16).ap()

        ident = sb("ident", [P, P])
        down = sb("down", [P, P])
        up = sb("up", [P, P])
        heads = sb("heads", [P, H])
        wk, wq, wm, w1, w2 = (sb(n, [P, D]) for n in ("wk", "wq", "wm", "w1", "w2"))
        bkc, bqc, b1c, b2c, gammac, betac = (sb(n, [P, 1]) for n in ("bkc", "bqc", "b1c", "b2c", "gammac", "betac"))
        bmr = sb("bmr", [P, D])
        b2r = sb("b2r", [P, D])
        epsc = sb("epsc", [P, 1])
        sign_i = sb("sign_i", [P, 2], I32)
        signs = sb("signs", [P, 6])
        turn = sb("turn", [P, 5, SORT])
        place = sb("place", [P, SORT])

        big = sb("big", [P, ROWS])
        dst_i = sb("dst_i", [P, TILES + 2 * U], I32)
        src_i = sb("src_i", [P, TILES + 2 * U], I32)
        out_i = sb("out_i", [P, TILES + 2 * U], I32)
        row_i = sb("row_i", [P, TILES + 2 * U], I32)
        stage = sb("stage", [P, 4, U], I32)
        rows = sb("rows", [P, 2, GW])
        ringA = sb("ringA", [P, 2, GW])
        ringB = sb("ringB", [P, 2, GW])
        zring = sb("zring", [P, 4, GW])
        flags = sb("flags", [P, 4, GW + 2], BF16)
        small = sb("small", [P, 2, U * H])
        sc = sb("sc", [P, TILES * H])
        gs = sb("gs", [P, H * TILES])
        sums = sb("sums", [P, 2, GROUPS])
        bn = sb("bn", [P, 12])
        rest = sb("rest", [P, D])
        many_i = sb("many_i", [1, 1], I32)
        late_i = sb("late_i", [1, 1], I32)
        lnst = sb("lnst", [P, 4, LR * 6])
        lnsm = sb("lnsm", [P, 4, 8, LR])

        room = sb("room", [P, ROOM])
        used = [0]

        def take(n):
            used[0] += n
            assert used[0] <= ROOM
            return room[:, used[0] - n:used[0]]

        va, vb, t1, t2 = (take(SORT) for _ in range(4))
        key, pay, key1 = (take(SORT) for _ in range(3))
        same1 = take(SORT + 1)
        same2 = take(SORT + 1)
        seqno = take(SORT).bitcast(I32)
        same16 = take(SORT // 2).bitcast(BF16)
        raw = take(2 * SORT).bitcast(I32)
        one_i = take(2).bitcast(I32)
        seg = take((H + 1) * SORT)
        fwd = take((H + 1) * SORT)
        bwd = take((H + 1) * SORT)
        negs = take(SORT)
        same_t = take(TILES)
        same_n = take(P + 1)
        pack = take(12)
        crow = take(2 * P)
        cscan = take(P + 2)
        carry = take(8)
        xin = [room[:, i * CW:(i + 1) * CW] for i in range(4)]
        final_rows = [rows[:, 0], rows[:, 1], ringB[:, 0], ringB[:, 1]]
        bound = sc[:, 0:TILES]
        ends = sc[:, TILES:2 * TILES]
        counted = sc[:, 2 * TILES:2 * TILES + 1]
        shared = sc[:, 2 * TILES + 1:2 * TILES + 2]

        PS = [ctx.enter_context(nc.psum_tensor(f"ps{i}", [P, 1024], F32)) for i in range(4)]

        pace = {n: sem(f"pace_{n}") for n in ("sp", "pool", "act", "dve", "pe")}
        lists_in, weights_in, biases_in = sem("lists_in"), sem("weights_in"), sem("biases_in")
        consts = sem("consts")
        raw_clear = sem("raw_clear")
        order_pe = sem("order_pe")
        order_dve = sem("order_dve")
        dve_step, act_step, pool_step = sem("dve_step"), sem("act_step"), sem("pool_step")
        sorted_keys = sem("sorted_keys")
        shifted = sem("shifted")
        marks = sem("marks")
        turned = sem("turned")
        indexed = sem("indexed")
        marks_out = sem("marks_out")
        kd_in = [sem(f"kd_in{h}") for h in range(2)]
        kd_saved = [sem(f"kd_saved{h}") for h in range(2)]
        kd_turned = sem("kd_turned")
        kx_ready = sem("kx_ready")
        k_made = sem("k_made")
        k_kept = sem("k_kept")
        qs_in = [sem(f"qs_in{h}") for h in range(2)]
        qs_turned = sem("qs_turned")
        qx_ready = sem("qx_ready")
        q_made = sem("q_made")
        qk_ready = sem("qk_ready")
        m_made = sem("m_made")
        m_kept = sem("m_kept")
        s_made = sem("s_made")
        s_kept = sem("s_kept")
        scores_out = sem("scores_out")
        g_in = [sem(f"g_in{h}") for h in range(2)]
        g_kept = sem("g_kept")
        soft_pe = sem("soft_pe")
        soft_dve = sem("soft_dve")
        soft_act = sem("soft_act")
        soft_exp = sem("soft_exp")
        narrowed = sem("narrowed")
        scores_taken = sem("scores_taken")
        weights_ready = sem("weights_ready")
        ones_made, ones_out = sem("ones_made"), sem("ones_out")
        a_out = [sem(f"a_out{h}") for h in range(2)]
        a_all = sem("a_all")
        a_in = sem("a_in")
        f_in = [sem(f"f_in{h}") for h in range(4)]
        o_made = sem("o_made")
        o_turned = sem("o_turned")
        run_sums = sem("run_sums")
        h_made = sem("h_made")
        h_kept = sem("h_kept")
        squares = sem("squares")
        bn_var = sem("bn_var")
        bn_sd = sem("bn_sd")
        bn_bias = sem("bn_bias")
        bn_rest = sem("bn_rest")
        rest_made = sem("rest_made")
        rest_ready = sem("rest_ready")
        d_in = [sem(f"d_in{i}") for i in range(4)]
        d_out = [sem(f"d_out{i}") for i in range(4)]
        l_var, l_sd, l_scale = (sem(f"l_{n}") for n in ("var", "sd", "scale"))
        d_done = sem("d_done")
        d_part = sem("d_part")
        late_pe, late_dve = sem("late_pe"), sem("late_dve")
        late_ready = sem("late_ready")
        kb_kept = sem("kb_kept")
        e_in = [sem(f"e_in{h}") for h in range(4)]
        e_relu = sem("e_relu")
        e_made = sem("e_made")
        e_done = sem("e_done")
        e_out = [sem(f"e_out{h}") for h in range(4)]

        def hold(eng, name, s, value):
            if isinstance(value, int):
                if value > 0:
                    eng.wait_ge(s, value)
            else:
                eng.wait_ge(s, value)
                eng.sem_inc(pace[name], 1)

        class Steps:

            def __init__(self, eng, name, s):
                self.eng, self.name, self.sem, self.n, self.local = eng, name, s, 0, 0

            def __call__(self, ins):
                ins.then_inc(self.sem, 1)
                self.local += 1

            def skip(self, n):
                self.settle()
                self.eng.sem_inc(self.sem, n)
                self.local += n

            def until(self, local):
                hold(self.eng, self.name, self.sem, self.n + local)

            def settle(self):
                hold(self.eng, self.name, self.sem, self.n + self.local)

            def loop(self, eng, first, last, body):
                self.n, self.local = self.n + self.local, 0
                start = self.n
                body(first)
                self.settle()
                once = self.local
                self.local = 0
                with eng.Fori(first + 1, last) as i:
                    self.n = start + once + (i - (first + 1)) * once
                    body(i)
                    self.settle()
                    assert self.local == once, (self.local, once)
                self.n, self.local = start + (last - first) * once, 0

        def group(t, g):
            return t[:, bass.ds(g * GW, GW)]

        block = ctx.enter_context(nc.Block())

        @block.sync
        def _(sp):
            sp.wait_ge(raw_clear, 1)
            for a, edges_ in ((0, dst), (SORT, src)):
                sp.dma_start(raw[0:LP, a:a + SORT],
                             edges_[0:LP * SORT].rearrange("(p n) -> p n", p=LP)).then_inc(lists_in, 16)
                sp.dma_start(raw[LP:LP + 1, a:a + E - LP * SORT],
                             edges_[LP * SORT:E].rearrange("(p n) -> p n", p=1)).then_inc(lists_in, 16)
            for t, w in ((wk, Wk), (wq, Wq), (wm, Wm), (w1, W1), (w2, W2)):
                sp.dma_start(t[:, :], w).then_inc(weights_in, 16)
            for t, b in ((bkc, bk), (bqc, bq), (b1c, b1), (b2c, b2), (gammac, gamma), (betac, beta)):
                sp.dma_start(t[:, :], b.rearrange("(p o) -> p o", o=1)).then_inc(biases_in, 16)
            for t, b in ((bmr, bm), (b2r, b2)):
                sp.dma_start(t[:, :], b.partition_broadcast(P)).then_inc(biases_in, 16)
            sp.wait_ge(ones_made, 1)
            sp.dma_start(alpha_d.rearrange("(p t) h -> p (t h)", p=P), gs[:, :]).then_inc(ones_out, 16)
            sp.wait_ge(indexed, 1)
            sp.dma_start(same_d.rearrange("(p n) -> p n", p=P), same16).then_inc(marks_out, 16)

            def save(i):
                for h in range(2):
                    hold(sp, "sp", kb_kept, 2 * i + h + 1)
                    sp.dma_start(xdst_d[bass.ds(2 * i + h, 1), :, :].rearrange("o p n -> (o p) n"),
                                 ringB[:, h, :]).then_inc(kd_saved[h], 16)
            save(0)
            with sp.Fori(1, PAIRS) as i:
                save(i)

            sp.wait_ge(s_kept, GROUPS)
            sp.dma_start(scores_d.rearrange("(p t) h -> p (t h)", p=P), sc[:, :]).then_inc(scores_out, 16)

            sp.wait_ge(marks_out, 16)

            def load_marks(i):
                for h in range(4):
                    g = 4 * i + h
                    hold(sp, "sp", h_kept, g - 3)
                    sp.dma_start(flags[:, h, 0:GW + 1],
                                 same_d[bass.ds(g * GW, GW + 1)].partition_broadcast(P)).then_inc(f_in[h], 16)
            load_marks(0)
            sp.wait_ge(a_all, 1)
            sp.dma_start(sc[:, :], alpha_d.rearrange("(p t) h -> p (t h)", p=P)).then_inc(a_in, 16)

            with sp.Fori(1, QUADS) as i:
                load_marks(i)

            sp.wait_ge(late_ready, 1)
            late = sp.value_load(late_i[0:1, 0:1], min_val=0, max_val=ROWS)
            sp.wait_ge(weights_ready, 1)

            def nodes(t, c):
                first = 0 if isinstance(c, int) and c == 0 else c * CHUNK - OVER
                return t[bass.ds(first, CHUNK), :].rearrange("(p n) d -> p (n d)", p=P)

            def store(c, k):
                hold(sp, "sp", d_done, c + 1)
                hold(sp, "sp", d_part, c + 1)
                sp.dma_start(nodes(y, c), xin[k]).then_inc(d_out[k], 16)

            def turns(i, dense, edge):
                for h in range(4):
                    s = 4 * i + h
                    if edge:
                        hold(sp, "sp", e_made, s - 3)
                        sp.dma_start(zring[:, h, :],
                                     xdst_d[bass.ds(s, 1), :, :].rearrange("o p n -> (o p) n")).then_inc(e_in[h], 16)
                    if dense:
                        hold(sp, "sp", d_out[h], i * 16)
                        sp.dma_start(xin[h], nodes(x, s)).then_inc(d_in[h], 16)
                        if not isinstance(s, int) or s >= LAG:
                            store(s - LAG, (h - LAG) % 4)

            def work(dense, edge):
                turns(0, dense, edge)
                with sp.Fori(1, QUADS) as i:
                    turns(i, dense, edge)
                if dense:
                    for c in range(CHUNKS - LAG, CHUNKS):
                        store(c, c % 4)

            with sp.If(late > 0):
                work(True, False)
                work(False, True)
            with sp.Else():
                work(True, True)
            for h in range(4):
                sp.wait_ge(d_out[h], 16 * QUADS)
                sp.wait_ge(e_out[h], 16 * U * QUADS)

        @block.gpsimd
        def _(pool):
            step = Steps(pool, "pool", pool_step)
            step(pool.memset(ident[:, :], 0.0))
            step(pool.memset(down[:, :], 0.0))
            step(pool.memset(up[:, :], 0.0))
            step(pool.memset(heads[:, :], 0.0))
            step(pool.memset(turn[:, :, :], 1.0))
            step(pool.memset(signs[:, :], 1.0))
            step(pool.memset(epsc[:, :], EPS))
            step(pool.iota(sign_i[:, 0:1], [[0, 1]], base=0, channel_multiplier=1))
            for index in (dst_i, src_i, out_i, row_i):
                step(pool.memset(index[:, TILES:TILES + 2 * U], 0))
            step(pool.iota(seqno, [[1, SORT]], base=0, channel_multiplier=SORT))
            step(pool.iota(place[:, :].bitcast(I32), [[1, 2], [TILES, P]], base=0, channel_multiplier=2))
            step(pool.iota(bound.bitcast(I32), [[CHUNK, GROUPS], [0, U]], base=CHUNK - OVER, channel_multiplier=0))
            step.settle()
            for m, base in ((ident, 0), (down, 1), (up, -1)):
                step(pool.affine_select(out=m[:, :], in_=m[:, :], compare_op=ALU.not_equal, fill=1.0, base=base,
                                        pattern=[[-1, P]], channel_multiplier=1))
            step.settle()
            for h in range(H):
                step(pool.memset(heads[DH * h:DH * h + DH, h:h + 1], 1.0 / math.sqrt(DH)))
                step.settle()
            for k in range(4):
                w = 2 ** k
                v = turn[:, k, :].rearrange("p (n q) -> p n q", q=4 * w)
                step(pool.memset(v[:, :, w:3 * w], -1.0))
            step(pool.memset(turn[:, 4, :].rearrange("p (n q) -> p n q", q=32)[:, :, 16:32], -1.0))
            step.settle()
            for q in range(4):
                b13, b14 = q & 1, q >> 1
                for col, s in ((1, b13), (2, b14), (3, b13 ^ b14)):
                    if s:
                        step(pool.memset(signs[32 * q:32 * q + 32, col:col + 1], -1.0))
                        step.settle()
            pool.sem_inc(consts, 1)

            def stream(index, free, issue, quads=QUADS):
                step(pool.tensor_copy(stage[:, 0:2, :].rearrange("p a u -> p (a u)"), index[:, 0:2 * U]))

                def groups(i):
                    for h in range(4):
                        g = 4 * i + h
                        free(g, h, i)
                        at = (h + 1) % 4
                        if h % 2:
                            step(pool.tensor_copy(stage[:, at:at + 2, :].rearrange("p a u -> p (a u)"),
                                                  index[:, bass.ds((g + 1) * U, 2 * U)]))
                        else:
                            step.settle()
                        issue(g, h, i, lambda k: bass.IndirectOffsetOnAxis(ap=stage[:, h, k:k + 1], axis=0))
                step.loop(pool, 0, quads, groups)

            def gather(table, index, out, width, done, free, quads=QUADS):
                def issue(g, h, i, at):
                    r = h % 2
                    for k in range(U):
                        pool.indirect_dma_start(out=out[:, r, k * width:(k + 1) * width], out_offset=None, in_=table,
                                                in_offset=at(k)).then_inc(done[r], 16)
                stream(index, free, issue, quads)

            pool.wait_ge(indexed, 1)
            gather(x[:, :], dst_i, rows, D, kd_in, lambda g, h, i: hold(pool, "pool", kd_turned, g - 1))

            pool.wait_ge(kd_turned, GROUPS)
            gather(x[:, :], src_i, rows, D, qs_in, lambda g, h, i: hold(pool, "pool", qs_turned, g - 1))

            pool.wait_ge(qs_turned, GROUPS)
            pool.wait_ge(late_ready, 1)
            late = pool.value_load(late_i[0:1, 0:1], min_val=0, max_val=ROWS)
            many = pool.value_load(many_i[0:1, 0:1], min_val=0, max_val=E)
            pool.wait_ge(indexed, 2)
            pool.wait_ge(scores_out, 16)

            def softmax(quads):
                gather(scores_d[:, :], row_i, small, H, g_in, lambda g, h, i: hold(pool, "pool", g_kept, g - 1), quads)
                pool.wait_ge(ones_out, 16)
                pool.wait_ge(weights_ready, 1)
                pool.wait_ge(g_kept, 4 * quads)

                def weights(g, h, i):
                    hold(pool, "pool", a_out[h % 2], (2 * i + h // 2) * 16 * U)
                    step(pool.tensor_copy(small[:, h % 2, :], gs[:, bass.ds(g * U * H, U * H)]))

                def scatter_weights(g, h, i, at):
                    step.settle()
                    for k in range(U):
                        pool.indirect_dma_start(out=alpha_d[:, :], out_offset=at(k),
                                                in_=small[:, h % 2, k * H:(k + 1) * H],
                                                in_offset=None).then_inc(a_out[h % 2], 16)
                stream(row_i, weights, scatter_weights, quads)
                for h in range(2):
                    pool.wait_ge(a_out[h], 16 * U * 2 * quads)
                pool.sem_inc(a_all, 1)

            before = step.n, step.local
            with pool.If(many > FEW * GW):
                softmax(QUADS)
            all_steps = step.n + step.local
            step.n, step.local = before
            with pool.Else():
                softmax(FEW // 4)
                step.skip(all_steps - step.n - step.local)

            def weigh(i):
                for h in range(2):
                    g = 2 * i + h
                    hold(pool, "pool", o_turned, g - 1)
                    pool.tensor_tensor(ringA[:, h, :].rearrange("p (n d) -> p n d", d=DH),
                                       group(big, g).rearrange("p (n d) -> p n d", d=DH),
                                       sc[:, bass.ds(g * U * H, U * H)].unsqueeze(2).to_broadcast([P, U * H, DH]),
                                       ALU.mult).then_inc(o_made, 1)
            pool.wait_ge(a_in, 16)
            pool.wait_ge(m_kept, GROUPS)
            weigh(0)
            with pool.Fori(1, PAIRS) as i:
                weigh(i)

            def reused(g, h, i):
                if h % 2:
                    for n in (1, 2):
                        hold(pool, "pool", e_out[(h + n) % 4], (i + (h == 3)) * 16 * U)

            def scatter(g, h, at):
                hold(pool, "pool", e_done, g + 1)
                for k in range(U):
                    pool.indirect_dma_start(out=y[:, :], out_offset=at(k), in_=final_rows[h][:, k * D:(k + 1) * D],
                                            in_offset=None, bounds_check=N - 1, oob_is_err=False).then_inc(e_out[h], 16)

            def scatter_stored(g, h, i, at):
                hold(pool, "pool", d_out[h], (i + 1) * 16)
                scatter(g, h, at)

            before = step.n, step.local
            with pool.If(late > 0):
                for h in range(4):
                    pool.wait_ge(d_out[h], 16 * QUADS)
                stream(out_i, reused, lambda g, h, i, at: scatter(g, h, at))
            step.n, step.local = before
            with pool.Else():
                stream(out_i, reused, scatter_stored)

        @block.scalar
        def _(act):
            step = Steps(act, "act", act_step)
            act.wait_ge(biases_in, 16 * 8)

            def keys(i):
                for h in range(2):
                    g = 2 * i + h
                    hold(act, "act", kd_turned, g + 1)
                    hold(act, "act", k_made, g - 1)
                    act.activation(ringA[:, h, :], PS[0][:, 0:GW], ACT.Identity).then_inc(kx_ready, 1)
                    hold(act, "act", kd_saved[h], i * 16)
                    hold(act, "act", kx_ready, g + 1)
                    act.activation(ringB[:, h, :], ringA[:, h, :], ACT.Identity, bias=b2c[:, 0:1]).then_inc(kb_kept, 1)
                    hold(act, "act", k_made, g + 1)
                    act.activation(group(big, g), PS[1][:, 0:GW], ACT.Identity, bias=bkc[:, 0:1]).then_inc(k_kept, 1)
            keys(0)
            with act.Fori(1, PAIRS) as i:
                keys(i)
            act.wait_ge(k_made, GROUPS)

            def scores(i):
                for h in range(2):
                    g = 2 * i + h
                    hold(act, "act", qs_turned, g + 1)
                    hold(act, "act", m_made, g - 1)
                    act.activation(ringA[:, h, :], PS[0][:, 0:GW], ACT.Identity).then_inc(qx_ready, 1)
            scores(0)
            with act.Fori(1, PAIRS) as i:
                scores(i)

            act.wait_ge(late_ready, 1)
            late = act.value_load(late_i[0:1, 0:1], min_val=0, max_val=ROWS)
            many = act.value_load(many_i[0:1, 0:1], min_val=0, max_val=E)
            act.wait_ge(soft_act, 1)
            with act.If(many > FEW * GW):
                act.activation(seg[0:SR, 0:H * SORT], bwd[0:SR, 0:H * SORT], ACT.Exp).then_inc(soft_exp, 1)
            with act.Else():
                act.activation(seg[0:FEW * U, 0:H * P], bwd[0:FEW * U, 0:H * P], ACT.Exp).then_inc(soft_exp, 1)

            step(act.activation(bn[:, 9:10], epsc[:, 0:1], ACT.Sqrt))
            def square(i):
                for h in range(2):
                    g = 2 * i + h
                    hold(act, "act", h_kept, g + 1)
                    step.settle()
                    step(act.activation(rows[:, h, :], group(big, g), ACT.Square,
                                        accum_out=sums[:, 1, bass.ds(g, 1)]))
                    act.sem_inc(pace["act"], 1)
            step.loop(act, 0, PAIRS, square)
            step.settle()
            act.sem_inc(squares, 1)

            act.wait_ge(bn_var, 1)
            act.activation(bn[:, 3:4], bn[:, 2:3], ACT.Sqrt, bias=epsc[:, 0:1]).then_inc(bn_sd, 1)
            act.wait_ge(bn_bias, 1)
            act.activation(bn[:, 8:9], bn[:, 7:8], ACT.Relu).then_inc(bn_rest, 1)

            def normalise(a, n, k, data, out, done):
                for j in range(n):
                    ins = act.activation(out[:, j * D:(j + 1) * D], data[:, j * D:(j + 1) * D], ACT.Identity,
                                         bias=lnsm[:, k, 6, a + j:a + j + 1], scale=lnsm[:, k, 5, a + j:a + j + 1])
                ins.then_inc(done, 1)

            def root(s, k, dense, edge, before):
                a, b = 0 if dense else CN, LR if edge else CN
                hold(act, "act", l_var, before + s + 1)
                act.activation(lnsm[:, k, 4, a:b], lnsm[:, k, 3, a:b], ACT.Sqrt, scale=1.0 / D,
                               bias=epsc[:, 0:1]).then_inc(l_sd, 1)

            def relu(g, h):
                hold(act, "act", e_made, g - 1)
                act.activation(ringA[:, h % 2, :], group(big, g), ACT.Relu, bias=bn[:, 7:8],
                               scale=bn[:, 5:6]).then_inc(e_relu, 1)

            def final(g, h, scattered, before):
                hold(act, "act", l_scale, before + g + 1)
                hold(act, "act", e_out[h], scattered * 16 * U)
                normalise(CN, U, h, PS[h], final_rows[h], e_done)

            def chunk_rows(c, h, before):
                hold(act, "act", l_scale, before + c + 1)
                normalise(0, CA, h, xin[h], xin[h], d_done)

            def turn_of(s, h, i, dense, edge, before):
                p2, p3 = (h - 2) % 4, (h - 3) % 4
                loop = not isinstance(s, int)
                two_ago = loop or 2 <= s < GROUPS + 2
                if two_ago:
                    root(s - 2, p2, dense, edge, before)
                if edge and (loop or s < GROUPS):
                    relu(s, h)
                if edge and (loop or s >= 3):
                    final(s - 3, p3, i - (h < 3), before)
                if dense and two_ago:
                    chunk_rows(s - 2, p2, before)

            def work(dense, edge, before):
                for h in range(4):
                    turn_of(h, h, 0, dense, edge, before)
                with act.Fori(1, QUADS) as i:
                    for h in range(4):
                        turn_of(4 * i + h, h, i, dense, edge, before)
                for h in range(3):
                    turn_of(GROUPS + h, h, QUADS, dense, edge, before)

            act.wait_ge(h_made, GROUPS)
            with act.If(late > 0):
                work(True, False, 0)
                work(False, True, CHUNKS)
            with act.Else():
                work(True, True, 0)

        @block.vector
        def _(dve):
            step = Steps(dve, "dve", dve_step)

            def two(view, w):
                return view.rearrange("p (n two s) -> p n two s", two=2, s=w)

            def exchange(a, b, w):
                ia, ib = two(a, w), two(b, w)
                step.settle()
                step(dve.tensor_tensor(ib[:, :, 0, :], ia[:, :, 0, :], ia[:, :, 1, :], ALU.min))
                step(dve.tensor_tensor(ib[:, :, 1, :], ia[:, :, 0, :], ia[:, :, 1, :], ALU.max))
                return b, a

            def mirror(a, b, w):
                ia, ib = two(a, w), two(b, w)
                step.settle()
                step(dve.tensor_tensor(ib[:, :, 0, :], ia[:, :, 0, :], ia[:, :, 1, ::-1], ALU.min))
                step(dve.tensor_tensor(ib[:, :, 1, :], ia[:, :, 0, ::-1], ia[:, :, 1, :], ALU.max))
                return b, a

            def sign(a, b, col):
                step.settle()
                step(dve.tensor_scalar(b, a, signs[:, col:col + 1], None, ALU.mult))
                return b, a

            def sort(a, b):
                a, b = sign(a, b, 0)
                for k in range(1, 9):
                    a, b = mirror(a, b, 2 ** (k - 1))
                    for j in range(k - 2, -1, -1):
                        a, b = exchange(a, b, 2 ** j)
                for k in range(9, 16):
                    step.settle()
                    step(dve.transpose(b, a))
                    a, b = b, a
                    if k < 14:
                        step.settle()
                        step(dve.tensor_tensor(b, a, turn[:, k - 9, :], ALU.mult))
                        a, b = b, a
                    if k == 13:
                        a, b = sign(a, b, 1)
                    if k == 14:
                        a, b = sign(a, b, 3)
                    if k == 15:
                        a, b = sign(a, b, 2)
                    for j in range(k - 1, 12, -1):
                        step.settle()
                        for q in range(4):
                            o = q ^ (1 << (j - 13))
                            s = -1.0 if (q >> (j - 13)) & 1 else 1.0
                            step(dve.tensor_scalar(b[32 * q:32 * q + 32, :], a[32 * o:32 * o + 32, :], s, None,
                                                   ALU.mult))
                        step.settle()
                        step(dve.scalar_tensor_tensor(t1, a, signs[:, j - 12:j - 11], b, ALU.mult, ALU.min))
                        step.settle()
                        step(dve.tensor_scalar(b, t1, signs[:, j - 12:j - 11], None, ALU.mult))
                        a, b = b, a
                    for j in range(min(k - 1, 12), 7, -1):
                        a, b = exchange(a, b, 2 ** (j - 8))
                    step.settle()
                    step(dve.transpose(b, a))
                    a, b = b, a
                    for j in range(7, -1, -1):
                        a, b = exchange(a, b, 2 ** j)
                step.settle()
                return a

            def high(values, tmp1, tmp2, out):
                step.settle()
                step(dve.tensor_scalar(tmp1, values, float(HALF), None, ALU.is_ge))
                step(dve.tensor_scalar(tmp2, values, 2.0, -float(2 * HALF + 32767), ALU.mult, ALU.add))
                step.settle()
                step(dve.tensor_tensor(tmp1, tmp1, tmp2, ALU.mult))
                step.settle()
                step(dve.tensor_scalar(tmp2, values, -1.0, float(HALF + 32895), ALU.mult, ALU.add))
                step.settle()
                step(dve.tensor_tensor(out, tmp1, tmp2, ALU.add))

            def unpack(v):
                lo, hi = v.bitcast(U16)[:, 0::2], v.bitcast(U16)[:, 1::2]
                step(dve.tensor_copy(pay, lo))
                step(dve.tensor_scalar(t1, hi, 32768.0, None, ALU.is_ge))
                step(dve.tensor_scalar(t2, hi, -2.0, float(2 * HALF + 32895 - HALF + 128 - HALF), ALU.mult, ALU.add))
                step(dve.tensor_scalar(key, hi, float(HALF - 128), None, ALU.add))
                step.settle()
                step(dve.tensor_tensor(t1, t1, t2, ALU.mult))
                step.settle()
                step(dve.tensor_tensor(key, key, t1, ALU.add))
                step.settle()
                step(dve.tensor_scalar(key1, key, 1.0, None, ALU.add))
                step.settle()

            def mark(same, n, only=None):
                dve.sem_inc(sorted_keys, 1)
                step(dve.tensor_tensor(same[:, 1:SORT], key1[:, 1:SORT], key1[:, 0:SORT - 1], ALU.is_equal))
                dve.wait_ge(shifted, 2 * n + 1)
                step(dve.tensor_tensor(same[:, 0:1], key1[:, 0:1], PS[2 * n][:, 0:1], ALU.is_equal))
                step.settle()
                if only is not None:
                    step(dve.tensor_tensor(same[:, 0:SORT], same[:, 0:SORT], only, ALU.mult))
                    step.settle()
                dve.sem_inc(marks, 1)
                dve.wait_ge(shifted, 2 * n + 2)
                step(dve.tensor_copy(same[:, SORT:SORT + 1], PS[2 * n][:, 2:3]))
                step.settle()

            step(dve.memset(raw, N))
            step.settle()
            dve.sem_inc(raw_clear, 1)
            dve.memset(gs[:, :], 1.0).then_inc(ones_made, 1)
            dve.wait_ge(consts, 1)
            step(dve.tensor_scalar(sign_i[:, 1:2], sign_i[:, 0:1], 1, None, ALU.bitwise_and))
            step.settle()
            step(dve.tensor_scalar(signs[:, 0:1], sign_i[:, 1:2], -2.0, 1.0, ALU.mult, ALU.add))
            dve.wait_ge(lists_in, 64)
            step(dve.tensor_copy(key, raw[:, 0:SORT]))
            step(dve.tensor_scalar(key1, raw[:, 0:SORT], 1.0, None, ALU.add))
            step(dve.tensor_copy(pay, raw[:, SORT:2 * SORT]))
            step.settle()
            dve.sem_inc(order_pe, 1)
            step(dve.tensor_tensor(t1[:, 1:SORT], key1[:, 1:SORT], key1[:, 0:SORT - 1], ALU.is_lt))
            dve.wait_ge(order_dve, 1)
            step(dve.tensor_tensor(t1[:, 0:1], key1[:, 0:1], PS[0][:, 0:1], ALU.is_lt))
            step.settle()
            step(dve.tensor_reduce(pack[:, 0:1], t1, AX.X, ALU.add))
            step.settle()
            dve.sem_inc(order_pe, 1)
            dve.wait_ge(order_dve, 2)
            step(dve.tensor_copy(one_i[0:1, 0:1], PS[0][0:1, 4:5]))
            step.settle()
            falls = dve.value_load(one_i[0:1, 0:1], min_val=0, max_val=E)
            before = step.local
            with dve.If(falls > 0):
                lo, hi = va.bitcast(U16)[:, 0::2], va.bitcast(U16)[:, 1::2]
                high(key, t1, t2, hi)
                step(dve.tensor_copy(lo, pay))
                v = sort(va, vb)
                unpack(v)
            with dve.Else():
                dve.sem_inc(dve_step, step.local - before)
            mark(same1, 0)
            step(dve.tensor_copy(same16, same1[:, 0:SORT]))
            step(dve.scalar_tensor_tensor(t2, same1[:, 1:SORT + 1], float(SKIP), key, ALU.mult, ALU.add))
            step.settle()
            dve.sem_inc(marks, 1)
            dve.wait_ge(turned, 1)
            for m, (dest, top) in enumerate(((dst_i, N - 1.0), (src_i, N - 1.0), (out_i, 2.0 * SKIP))):
                psv = PS[m][:, 0:2 * P].rearrange("p (c t) -> p c t", c=2)[:, :, 0:SR]
                step(dve.tensor_scalar(dest[:, 0:TILES].rearrange("p (t c) -> p c t", c=2), psv, top, None, ALU.min))
            step.settle()
            dve.sem_inc(indexed, 1)

            step(dve.tensor_copy(bound, bound.bitcast(I32)))
            step(dve.tensor_copy(ends, dst_i[:, 0:TILES]))
            step.settle()
            step(dve.tensor_tensor(ends, ends, bound, ALU.is_ge))
            step.settle()
            step(dve.tensor_reduce(counted, ends[:, 0:TILES - U], AX.X, ALU.add))
            step.settle()
            dve.sem_inc(late_pe, 1)

            step(dve.tensor_copy(t1, place[:, :].bitcast(I32)))
            step.settle()
            step(dve.tensor_copy(key, pay))
            step(dve.tensor_scalar(t2[:, 0:1], sign_i[:, 0:1], float(SR), None, ALU.is_ge))
            step.settle()
            step(dve.tensor_scalar(t2[:, 0:1], t2[:, 0:1], float(ROWS), None, ALU.mult))
            step.settle()
            v0 = va if v is vb else vb
            other = v
            lo, hi = v0.bitcast(U16)[:, 0::2], v0.bitcast(U16)[:, 1::2]
            step(dve.tensor_scalar(lo, t1, t2[:, 0:1], None, ALU.add))
            step.settle()
            high(key, t1, t2, hi)
            v = sort(v0, other)
            unpack(v)
            step(dve.tensor_scalar(t2, key, float(N), None, ALU.is_lt))
            step.settle()
            mark(same2, 1, t2)
            step(dve.tensor_tensor(t1, same2[:, 0:SORT], same2[:, 1:SORT + 1], ALU.max))
            step(dve.tensor_copy(key, seqno))
            step.settle()
            step(dve.tensor_reduce(shared, t1, AX.X, ALU.add))
            step.settle()
            step(dve.tensor_scalar(t1, t1, -float(E), float(E), ALU.mult, ALU.add))
            step.settle()
            dve.sem_inc(late_pe, 1)
            step(dve.tensor_tensor(key, key, t1, ALU.add))
            step(dve.tensor_scalar(pay, pay, 32767.0, None, ALU.min))
            step.settle()
            step(dve.tensor_scalar(key, key, float(N), None, ALU.min))
            free = va if v is vb else vb
            lo, hi = free.bitcast(U16)[:, 0::2], free.bitcast(U16)[:, 1::2]
            step(dve.scalar_tensor_tensor(lo, same2[:, 0:SORT], 32768.0, pay, ALU.mult, ALU.add))
            step.settle()
            high(key, t1, t2, hi)
            w = sort(free, v)
            step(dve.tensor_copy(pay, w.bitcast(U16)[:, 0::2]))
            step.settle()
            step(dve.tensor_scalar(same2[:, 0:SORT], pay, 32768.0, None, ALU.is_ge))
            step.settle()
            step(dve.scalar_tensor_tensor(pay, same2[:, 0:SORT], -32768.0, pay, ALU.mult, ALU.add))
            step.settle()
            dve.sem_inc(marks, 1)
            dve.wait_ge(shifted, 5)
            step(dve.tensor_copy(same2[:, SORT:SORT + 1], PS[2][:, 2:3]))
            step.settle()
            dve.sem_inc(marks, 1)
            dve.wait_ge(late_dve, 2)
            step(dve.tensor_copy(late_i[0:1, 0:1], PS[3][0:1, 0:1]))
            step(dve.tensor_copy(many_i[0:1, 0:1], PS[3][0:1, 1:2]))
            step.settle()
            dve.sem_inc(late_ready, 1)
            late = dve.value_load(late_i[0:1, 0:1], min_val=0, max_val=ROWS)
            many = dve.value_load(many_i[0:1, 0:1], min_val=0, max_val=E)
            dve.wait_ge(turned, 2)
            for m, to in enumerate((row_i[:, 0:TILES], same_t)):
                psv = PS[m][:, 0:2 * P].rearrange("p (c t) -> p c t", c=2)[:, :, 0:SR]
                step(dve.tensor_scalar(to.rearrange("p (t c) -> p c t", c=2), psv, ROWS - 1.0, None, ALU.min))
            step.settle()
            dve.sem_inc(indexed, 1)
            dve.wait_ge(narrowed, 1)
            step(dve.tensor_copy(same_n[0:FEW * U, 0:P], PS[2][0:FEW * U, 0:P]))
            step.settle()
            dve.sem_inc(marks, 1)
            dve.wait_ge(narrowed, 2)
            dve.tensor_copy(same_n[0:FEW * U, P:P + 1], PS[2][0:FEW * U, P:P + 1]).then_inc(marks, 1)
            dve.wait_ge(marks, 7)

            def scores(i):
                for h in range(2):
                    g = 2 * i + h
                    hold(dve, "dve", q_made, g + 1)
                    hold(dve, "dve", s_made, g - 1)
                    dve.scalar_tensor_tensor(ringB[:, h, :], PS[1][:, 0:GW], bqc[:, 0:1], group(big, g),
                                             ALU.add, ALU.mult).then_inc(qk_ready, 1)
                    hold(dve, "dve", m_made, g + 1)
                    hold(dve, "dve", qk_ready, g + 1)
                    dve.tensor_tensor(group(big, g).rearrange("p (n d) -> p n d", d=D),
                                      PS[2][:, 0:GW].rearrange("p (n d) -> p n d", d=D),
                                      bmr[:, :].unsqueeze(1).to_broadcast([P, U, D]), ALU.add).then_inc(m_kept, 1)
                    hold(dve, "dve", s_made, g + 1)
                    dve.tensor_copy(sc[:, bass.ds(g * U * H, U * H)], PS[3][:, 0:U * H]).then_inc(s_kept, 1)
            dve.wait_ge(k_kept, GROUPS)
            for h in range(2):
                dve.wait_ge(kd_saved[h], 16 * PAIRS)
            dve.wait_ge(biases_in, 16 * 8)
            scores(0)
            with dve.Fori(1, PAIRS) as i:
                scores(i)

            def softmax(R, W, same, quads):
                sp_, sn_ = same[0:R, 0:W], same[0:R, 1:W + 1]
                K = H + 1
                segv = seg[0:R, 0:K * W].rearrange("p (j f) -> p j f", j=K)
                fwdv = fwd[0:R, 0:K * W].rearrange("p (j f) -> p j f", j=K)
                bwdv = bwd[0:R, 0:K * W].rearrange("p (j f) -> p j f", j=K)
                ng = negs[0:R, 0:W]
                whole_before, whole_low, whole_after = (pack[0:R, j:j + 1] for j in (9, 10, 11))
                turn_no = [0]

                def cross(a, b, back, last, whole, start, op0, op1):
                    n = b - a
                    step.settle()
                    step(dve.tensor_copy(pack[0:R, 0:n].unsqueeze(2), last))
                    step(dve.tensor_copy(pack[0:R, H:H + n], whole.to_broadcast([R, n])))
                    step(dve.memset(cscan[0:n, R:R + 1] if back else cscan[0:n, 0:1], start))
                    step.settle()
                    dve.sem_inc(soft_pe, 1)
                    turn_no[0] += 1
                    dve.wait_ge(soft_dve, turn_no[0])
                    step(dve.tensor_copy(crow[0:n, :].rearrange("p (a n) -> p a n", a=2)[:, :, 0:R],
                                         PS[3][0:n, 0:2 * P].rearrange("p (a n) -> p a n", a=2)[:, :, 0:R]))
                    step.settle()
                    m, v = crow[0:n, P:P + R], crow[0:n, 0:R]
                    if back:
                        step(dve.tensor_tensor_scan(cscan[0:n, 0:R][:, ::-1], m[:, ::-1], v[:, ::-1], start, op0, op1))
                    else:
                        step(dve.tensor_tensor_scan(cscan[0:n, 1:R + 1], m, v, start, op0, op1))
                    step.settle()
                    dve.sem_inc(soft_pe, 1)
                    turn_no[0] += 1
                    dve.wait_ge(soft_dve, turn_no[0])
                    step(dve.tensor_copy(carry[0:R, 0:n], PS[3][0:R, 512:512 + n]))
                    step.settle()

                def forward(a, b, mask, start, op0, op1, whole):
                    step.settle()
                    for j in range(a, b):
                        step(dve.tensor_tensor_scan(fwdv[:, j, :], mask, segv[:, j, :], start, op0, op1))
                    cross(a, b, False, fwdv[:, a:b, W - 1:W], whole, start, op0, op1)
                    for j in range(a, b):
                        step(dve.tensor_tensor_scan(fwdv[:, j, :], mask, segv[:, j, :], carry[0:R, j - a:j - a + 1],
                                                    op0, op1))
                    step.settle()

                def backward(a, b):
                    for j in range(a, b):
                        step(dve.scalar_tensor_tensor(fwdv[:, j, :], sn_, 0.0, fwdv[:, j, :], ALU.is_equal, ALU.mult))
                    step.settle()
                    for j in range(a, b):
                        step(dve.tensor_tensor_scan(bwdv[:, j, ::-1], sn_[:, ::-1], fwdv[:, j, ::-1], 0.0,
                                                    ALU.mult, ALU.add))
                    cross(a, b, True, bwdv[:, a:b, 0:1], whole_after, 0.0, ALU.mult, ALU.add)
                    for j in range(a, b):
                        step(dve.tensor_tensor_scan(bwdv[:, j, ::-1], sn_[:, ::-1], fwdv[:, j, ::-1],
                                                    carry[0:R, j - a:j - a + 1], ALU.mult, ALU.add))
                    step.settle()

                step(dve.tensor_scalar(ng, sp_, 1.0, -LOW, ALU.subtract, ALU.mult))
                step(dve.memset(segv[:, H, :], 1.0))
                step(dve.tensor_reduce(whole_before, sp_, AX.X, ALU.min))
                step(dve.tensor_reduce(whole_after, sn_, AX.X, ALU.min))
                step.settle()
                step(dve.tensor_scalar(whole_low, whole_before, 1.0, -LOW, ALU.subtract, ALU.mult))
                forward(H, K, sp_, 0.0, ALU.mult, ALU.add, whole_before)
                backward(H, K)

                def take_scores(i):
                    for h in range(2):
                        g = 2 * i + h
                        hold(dve, "dve", g_in[h], (i + 1) * 16 * U)
                        dve.tensor_copy(gs[:, :].rearrange("p (h t) -> p h t", h=H)[:, :, bass.ds(g * U, U)],
                                        small[:, h, :].rearrange("p (t h) -> p h t", h=H)).then_inc(g_kept, 1)

                def take_all(pairs):
                    take_scores(0)
                    with dve.Fori(1, pairs) as i:
                        take_scores(i)
                    dve.wait_ge(g_kept, 2 * pairs)
                    dve.sem_inc(scores_taken, 1)
                step.settle()
                dve.wait_ge(ones_out, 16)
                take_all(4 * quads // 2)
                turn_no[0] += 1
                dve.wait_ge(soft_dve, turn_no[0])
                step(dve.tensor_copy(seg[0:R, 0:H * W], PS[0][0:R, 0:H * W]))
                forward(0, H, ng, LOW, ALU.add, ALU.max, whole_low)
                backward(0, H)
                step(dve.tensor_tensor(bwd[0:R, 0:H * W], seg[0:R, 0:H * W], bwd[0:R, 0:H * W], ALU.subtract))
                step.settle()
                dve.sem_inc(soft_act, 1)
                dve.wait_ge(soft_exp, 1)
                forward(0, H, sp_, 0.0, ALU.mult, ALU.add, whole_before)
                backward(0, H)
                for j in range(H):
                    step(dve.reciprocal(fwdv[:, j, :], bwdv[:, j, :]))
                    step(dve.tensor_tensor(segv[:, j, :], segv[:, j, :], bwdv[:, H, :], ALU.mult))
                step.settle()
                step(dve.tensor_tensor(seg[0:R, 0:H * W], seg[0:R, 0:H * W], fwd[0:R, 0:H * W], ALU.mult))
                step.settle()
                dve.sem_inc(soft_pe, 1)
                turn_no[0] += 1
                dve.wait_ge(soft_dve, turn_no[0])
                parts = W // P
                for c in range(parts):
                    step(dve.tensor_copy(gs[:, 0:R * parts * H].rearrange("p (t c h) -> p c h t", c=parts, h=H)[:, c],
                                         PS[1][:, 512 * c:512 * c + H * P].rearrange("p (h t) -> p h t", h=H)[:, :, 0:R]))
                step.settle()
                dve.sem_inc(weights_ready, 1)

            before = step.n, step.local
            with dve.If(many > FEW * GW):
                softmax(SR, SORT, same2, QUADS)
            all_steps = step.n + step.local
            step.n, step.local = before
            with dve.Else():
                softmax(FEW * U, P, same_n, FEW // 4)
                step.skip(all_steps - step.n - step.local)

            def scan(g, h, i):
                hold(dve, "dve", o_turned, g + 1)
                hold(dve, "dve", f_in[h], i * 16)
                hold(dve, "dve", h_made, g - 1)
                hold(dve, "dve", run_sums, g)
                first = isinstance(g, int) and g == 0
                r = h % 2
                dve.tensor_tensor_scan(ringB[:, r, :], flags[:, h, 0:GW], PS[2 * r][:, 0:GW],
                                       0.0 if first else ringB[:, 1 - r, GW - 1:GW],
                                       ALU.mult, ALU.add).then_inc(run_sums, 1)

            def keep(g, h):
                hold(dve, "dve", h_made, g + 1)
                dve.scalar_tensor_tensor(group(big, g), flags[:, h, 1:GW + 1], 0.0, PS[2 * (h % 2) + 1][:, 0:GW],
                                         ALU.is_equal, ALU.mult,
                                         accum_out=sums[:, 0, bass.ds(g, 1)]).then_inc(h_kept, 1)

            def run_group(i):
                for h in range(4):
                    g = 4 * i + h
                    if not isinstance(g, int) or g > 0:
                        scan(g - 1, (h - 1) % 4, i + (h > 0))
                    if not isinstance(g, int) or g > 1:
                        keep(g - 2, (h - 2) % 4)
            run_group(0)
            with dve.Fori(1, QUADS) as i:
                run_group(i)
            scan(GROUPS - 1, 3, QUADS)
            keep(GROUPS - 2, 2)
            keep(GROUPS - 1, 3)

            dve.wait_ge(squares, 1)
            dve.wait_ge(h_kept, GROUPS)
            step(dve.tensor_reduce(bn[:, 0:2], sums[:, :, :], AX.X, ALU.add))
            step.settle()
            step(dve.tensor_scalar(bn[:, 0:2], bn[:, 0:2], 1.0 / N, None, ALU.mult))
            step.settle()
            step(dve.tensor_tensor(bn[:, 4:5], bn[:, 0:1], bn[:, 0:1], ALU.mult))
            step(dve.tensor_tensor(bn[:, 6:7], bn[:, 0:1], b1c[:, 0:1], ALU.add))
            step.settle()
            step(dve.tensor_tensor(bn[:, 2:3], bn[:, 1:2], bn[:, 4:5], ALU.subtract))
            step.settle()
            dve.sem_inc(bn_var, 1)
            dve.wait_ge(bn_sd, 1)
            step(dve.reciprocal(bn[:, 4:5], bn[:, 3:4]))
            step(dve.tensor_tensor(bn[:, 6:7], b1c[:, 0:1], bn[:, 6:7], ALU.subtract))
            step.settle()
            step(dve.tensor_tensor(bn[:, 5:6], bn[:, 4:5], gammac[:, 0:1], ALU.mult))
            step.settle()
            step(dve.scalar_tensor_tensor(bn[:, 7:8], bn[:, 6:7], bn[:, 5:6], betac[:, 0:1], ALU.mult, ALU.add))
            step.settle()
            dve.sem_inc(bn_bias, 1)
            dve.wait_ge(rest_made, 1)
            step(dve.tensor_tensor(rest[:, :], PS[2][:, 0:D], b2r[:, :], ALU.add))
            step.settle()
            dve.sem_inc(rest_ready, 1)

            def bn_rows(k, at, data, a, b):
                for j in range(a, b):
                    r = 6 * (at + j)
                    step(dve.bn_stats(lnst[:, k, r:r + 6], data[:, j * D:(j + 1) * D]))

            def turn_of(s, h, i, dense, edge, before):
                some = not isinstance(s, int) or s > 0
                going = not isinstance(s, int) or s < CHUNKS
                p = (h - 1) % 4
                a, b = 0 if dense else CN, LR if edge else CN
                q = lnsm[:, p, :, a:b]
                st = lnst[:, p, 6 * a:6 * b].rearrange("p (n s) -> p n s", s=6)
                base = step.local

                def small(n, body, after=None):
                    if not some:
                        step.skip(n)
                        return step.local
                    if after is not None:
                        step.until(after)
                    at = step.local
                    body()
                    assert step.local == at + n
                    return step.local

                def halves():
                    step(dve.tensor_tensor(q[:, 0, :], st[:, :, 1], st[:, :, 4], ALU.add))
                    step(dve.tensor_tensor(q[:, 1, :], st[:, :, 1], st[:, :, 4], ALU.subtract))
                    step(dve.tensor_tensor(q[:, 2, :], st[:, :, 2], st[:, :, 5], ALU.add))

                def square():
                    step(dve.tensor_tensor(q[:, 1, :], q[:, 1, :], q[:, 1, :], ALU.mult))

                def inverse():
                    if dense:
                        hold(dve, "dve", d_done, s - 4)
                    if edge:
                        hold(dve, "dve", e_done, s - 4)
                    hold(dve, "dve", l_sd, before + s)
                    step(dve.reciprocal(q[:, 5, :], q[:, 4, :]))

                def share():
                    hold(dve, "dve", l_scale, before + s)
                    for j in range(CA, CN):
                        row = xin[p][:, j * D:(j + 1) * D]
                        ins = dve.tensor_scalar(row, row, lnsm[:, p, 5, j:j + 1], lnsm[:, p, 6, j:j + 1],
                                                ALU.mult, ALU.add)
                        if j < CN - 1:
                            step(ins)
                    ins.then_inc(d_part, 1)

                if dense and going:
                    hold(dve, "dve", d_in[h], (i + 1) * 16)
                    v = xin[h].rearrange("p (n d) -> p n d", d=D)
                    step(dve.tensor_tensor(v, v, rest[:, :].unsqueeze(1).to_broadcast([P, CN, D]), ALU.add))
                added = step.local
                halved = small(3, halves, base)
                if dense and going:
                    step.until(added)
                    bn_rows(h, 0, xin[h], 0, 2)
                squared = small(1, square, halved)
                if dense and going:
                    bn_rows(h, 0, xin[h], 2, 4)
                if some:
                    step.until(squared)
                    dve.scalar_tensor_tensor(q[:, 3, :], q[:, 1, :], D / 4.0, q[:, 2, :],
                                             ALU.mult, ALU.add).then_inc(l_var, 1)
                if dense and going:
                    bn_rows(h, 0, xin[h], 4, CN)
                if edge and going:
                    hold(dve, "dve", e_made, s + 1)
                    bn_rows(h, CN, PS[h], 0, 4)
                inverted = small(1, inverse)
                if edge and going:
                    bn_rows(h, CN, PS[h], 4, U)
                if some:
                    step.until(inverted)
                    dve.scalar_tensor_tensor(q[:, 6, :], q[:, 0, :], -0.5, q[:, 5, :],
                                             ALU.mult, ALU.mult).then_inc(l_scale, 1)
                if dense:
                    small(CN - CA - 1, share)

            def work(dense, edge, before):
                def turns(i):
                    for h in range(4):
                        turn_of(4 * i + h, h, i, dense, edge, before)
                step.loop(dve, 0, QUADS, turns)
                step.settle()
                turn_of(CHUNKS, 0, QUADS, dense, edge, before)
                step.settle()

            before = step.n, step.local
            with dve.If(late > 0):
                work(True, False, 0)
                work(False, True, CHUNKS)
            step.n, step.local = before
            with dve.Else():
                work(True, True, 0)

        @block.tensor
        def _(pe):
            pe.wait_ge(consts, 1)

            def wide(out, w, data):
                pe.matmul(out[:, 0:512], w[:, :], data[:, 0:512], start=True, stop=True)
                return pe.matmul(out[:, 512:GW], w[:, :], data[:, 512:GW], start=True, stop=True)

            def flip(out, data):
                for k in range(U):
                    last = pe.transpose(out[:, k * P:(k + 1) * P], data[:, k * P:(k + 1) * P], ident[:, :])
                return last

            def borders(n):
                pe.wait_ge(sorted_keys, n + 1)
                pe.matmul(PS[2 * n][:, 0:1], down[:, :], key1[:, SORT - 1:SORT], start=True, stop=True)\
                  .then_inc(shifted, 1)
                pe.wait_ge(marks, 2 * n + 1)
                pe.matmul(PS[2 * n][:, 2:3], up[:, :], (same1, same2)[n][:, 0:1], start=True, stop=True)\
                  .then_inc(shifted, 1)

            def by_tiles(arrays):
                for m, t in enumerate(arrays):
                    for c in range(2):
                        last = pe.transpose(PS[m][:, c * P:(c + 1) * P], t[:, c * P:(c + 1) * P], ident[:, :])
                last.then_inc(turned, 1)

            pe.wait_ge(order_pe, 1)
            pe.matmul(PS[0][:, 0:1], down[:, :], key1[:, SORT - 1:SORT], start=True, stop=True).then_inc(order_dve, 1)
            pe.wait_ge(order_pe, 2)
            pe.matmul(PS[0][0:1, 4:5], pack[:, 0:1], signs[:, 4:5], start=True, stop=True).then_inc(order_dve, 1)

            borders(0)
            pe.wait_ge(marks, 2)
            by_tiles((key, pay, t2))
            pe.wait_ge(indexed, 1)
            pe.wait_ge(weights_in, 16 * 5)

            def keys(i):
                for h in range(2):
                    g = 2 * i + h
                    hold(pe, "pe", kd_in[h], (i + 1) * 16 * U)
                    hold(pe, "pe", kx_ready, g)
                    flip(PS[0], rows[:, h, :]).then_inc(kd_turned, 1)
                    hold(pe, "pe", kx_ready, g + 1)
                    hold(pe, "pe", k_kept, g)
                    wide(PS[1], wk, ringA[:, h, :]).then_inc(k_made, 1)
            keys(0)
            with pe.Fori(1, PAIRS // 2) as i:
                keys(i)
            borders(1)
            with pe.Fori(PAIRS // 2, PAIRS) as i:
                keys(i)
            pe.wait_ge(late_pe, 1)
            pe.matmul(PS[3][0:1, 0:1], counted, signs[:, 4:5], start=True, stop=True).then_inc(late_dve, 1)
            pe.wait_ge(late_pe, 2)
            pe.matmul(PS[3][0:1, 1:2], shared, signs[:, 4:5], start=True, stop=True).then_inc(late_dve, 1)
            pe.wait_ge(marks, 4)
            pe.matmul(PS[2][:, 2:3], up[:, :], same2[:, 0:1], start=True, stop=True).then_inc(shifted, 1)
            pe.wait_ge(marks, 5)
            pe.wait_ge(kx_ready, GROUPS)
            pe.wait_ge(k_kept, GROUPS)
            by_tiles((pay, same2))
            pe.wait_ge(indexed, 2)
            pe.transpose(PS[2][0:FEW * U, 0:P], same_t[:, 0:FEW * U], ident[:, :]).then_inc(narrowed, 1)
            pe.wait_ge(marks, 6)
            pe.matmul(PS[2][0:FEW * U, P:P + 1], up[0:FEW * U, 0:FEW * U], same_n[0:FEW * U, 0:1],
                      start=True, stop=True).then_inc(narrowed, 1)
            pe.wait_ge(marks, 7)

            def flip_rows(g, h, arrived):
                hold(pe, "pe", qs_in[h], arrived * 16 * U)
                hold(pe, "pe", qx_ready, g)
                flip(PS[0], rows[:, h, :]).then_inc(qs_turned, 1)

            def scores(i):
                for h in range(2):
                    g = 2 * i + h
                    hold(pe, "pe", qx_ready, g + 1)
                    hold(pe, "pe", qk_ready, g)
                    wide(PS[1], wq, ringA[:, h, :]).then_inc(q_made, 1)
                    hold(pe, "pe", m_kept, g)
                    for k in range(U):
                        last = pe.matmul(PS[2][:, k * D:(k + 1) * D], ringA[:, h, k * P:(k + 1) * P], wm[:, :],
                                         start=True, stop=True)
                    last.then_inc(m_made, 1)
                    if not isinstance(g, int) or g < GROUPS - 1:
                        flip_rows(g + 1, 1 - h, i + 1 + h)
                    hold(pe, "pe", qk_ready, g + 1)
                    hold(pe, "pe", s_kept, g)
                    for k in range(U):
                        last = pe.matmul(PS[3][:, k * H:(k + 1) * H], ringB[:, h, k * P:(k + 1) * P], heads[:, :],
                                         start=True, stop=True)
                    last.then_inc(s_made, 1)
            flip_rows(0, 0, 1)
            scores(0)
            with pe.Fori(1, PAIRS - 1) as i:
                scores(i)
            scores(PAIRS - 1)

            def softmax(R, W):
                asked = [0]

                def cross(n, back):
                    asked[0] += 1
                    pe.wait_ge(soft_pe, asked[0])
                    pe.transpose(PS[3][0:n, 0:R], pack[0:R, 0:n], ident[0:R, 0:R])
                    pe.transpose(PS[3][0:n, P:P + R], pack[0:R, H:H + n], ident[0:R, 0:R]).then_inc(soft_dve, 1)
                    asked[0] += 1
                    pe.wait_ge(soft_pe, asked[0])
                    at = 1 if back else 0
                    pe.transpose(PS[3][0:R, 512:512 + n], cscan[0:n, at:at + R],
                                 ident[0:n, 0:n]).then_inc(soft_dve, 1)

                cross(1, False)
                cross(1, True)
                pe.wait_ge(scores_taken, 1)
                parts = W // P
                for h in range(H):
                    for c in range(parts):
                        at = h * TILES
                        last = pe.transpose(PS[0][0:R, h * W + c * P:h * W + (c + 1) * P],
                                            gs[:, at:at + R * parts].rearrange("p (t c) -> p c t", c=parts)[:, c, :],
                                            ident[:, :])
                last.then_inc(soft_dve, 1)
                for back in (False, True, False, True):
                    cross(H, back)
                pe.wait_ge(soft_pe, asked[0] + 1)
                for h in range(H):
                    for c in range(parts):
                        last = pe.transpose(PS[1][:, 512 * c + h * P:512 * c + h * P + R],
                                            seg[0:R, h * W + c * P:h * W + (c + 1) * P], ident[0:R, 0:R])
                last.then_inc(soft_dve, 1)

            pe.wait_ge(s_kept, GROUPS)
            pe.wait_ge(late_ready, 1)
            many = pe.value_load(many_i[0:1, 0:1], min_val=0, max_val=E)
            with pe.If(many > FEW * GW):
                softmax(SR, SORT)
            with pe.Else():
                softmax(FEW * U, P)

            def flip_sums(g, h):
                hold(pe, "pe", o_made, g + 1)
                hold(pe, "pe", run_sums, g - 1)
                flip(PS[2 * h], ringA[:, h, :]).then_inc(o_turned, 1)

            def first_layer(g, h):
                hold(pe, "pe", run_sums, g + 1)
                hold(pe, "pe", h_kept, g - 1)
                wide(PS[2 * h + 1], w1, ringB[:, h, :]).then_inc(h_made, 1)

            flip_sums(0, 0)
            flip_sums(1, 1)
            first_layer(0, 0)
            with pe.Fori(1, PAIRS) as i:
                for h in range(2):
                    g = 2 * i + h
                    flip_sums(g, h)
                    first_layer(g - 1, 1 - h)
            first_layer(GROUPS - 1, 1)

            pe.wait_ge(bn_rest, 1)
            pe.matmul(PS[2][:, 0:D], bn[:, 8:9].to_broadcast([P, P]), w2[:, :], start=True, stop=True)\
              .then_inc(rest_made, 1)

            def edges(i):
                for h in range(4):
                    g = 4 * i + h
                    hold(pe, "pe", e_relu, g + 1)
                    hold(pe, "pe", e_in[h], (i + 1) * 16)
                    hold(pe, "pe", e_done, g - 3)
                    for k in range(U):
                        out = PS[h][:, k * D:(k + 1) * D]
                        pe.matmul(out, ringA[:, h % 2, k * P:(k + 1) * P], w2[:, :], start=True, stop=False)
                        last = pe.matmul(out, zring[:, h, k * P:(k + 1) * P], ident[:, :], start=False, stop=True)
                    last.then_inc(e_made, 1)
            pe.wait_ge(rest_ready, 1)
            edges(0)
            with pe.Fori(1, QUADS) as i:
                edges(i)


_NAMES = ["x", "src", "dst", "L0_gnn_Wk", "L0_gnn_bk", "L0_gnn_Wm", "L0_gnn_bm", "L0_gnn_Wq", "L0_gnn_bq",
          "L0_gnn_W1", "L0_gnn_b1", "L0_gnn_gamma", "L0_gnn_beta", "L0_gnn_W2", "L0_gnn_b2"]


def kernel(**inputs):
    import numpy as np
    import concourse.bacc as bacc
    from concourse.bass_utils import run_bass_kernel_spmd as run

    nc = bacc.Bacc("TRN2", target_bir_lowering=False, num_devices=1)
    arrays, args = {}, []
    for name in _NAMES:
        a = np.ascontiguousarray(inputs[name])
        arrays[f"in_{name}"] = a
        args.append(nc.dram_tensor(f"in_{name}", a.shape, mybir.dt.from_np(a.dtype), kind="ExternalInput").ap())
    y = nc.dram_tensor("y", (N, D), F32, kind="ExternalOutput").ap()
    build(nc, *args, y)
    return run(nc, [arrays], core_ids=[0]).results[0]["y"]
```
